# Optimizing a Trainium2 kernel written in Bass

```python
import numpy as np
import jax
import jax.numpy as jnp

def _softmax(x, axis=-1):
    return jax.nn.softmax(x, axis=axis)

def _gelu(x):
    return jax.nn.gelu(x, approximate=True)

def _silu(x):
    return jax.nn.silu(x)

def _sigmoid(x):
    return jax.nn.sigmoid(x)

def _layernorm(x, axis=-1, eps=1e-05):
    m = jnp.mean(x, axis=axis, keepdims=True)
    v = jnp.var(x, axis=axis, keepdims=True)
    return (x - m) / jnp.sqrt(v + eps)

def _scatter_add(tgt, idx, src, axis=0):
    return tgt.at[idx].add(src)

def _segment_sum(src, seg, n):
    return jax.ops.segment_sum(src, seg, n)
kernel_name = 'mk_cond_resid_d2_seqx_r2_6cd944'

def setup_inputs(seed: int=0):
    np.random.seed(seed)
    _w = jnp.asarray

    def _rec_inputs():
        import jax
        import jax.numpy as jnp
        _rk = jax.random.key(seed)
        x = -0.000125 + 0.9999 * jax.random.normal(jax.random.fold_in(_rk, 1), (128, 128, 512), jnp.float32)
        _lenS = 128 - jax.random.randint(jax.random.fold_in(_rk, 7), (128,), 0, max(1, 128 // 4) + 1, jnp.int32)
        _lenS2 = 128 - jax.random.randint(jax.random.fold_in(_rk, 8), (128,), 0, max(1, 128 // 4) + 1, jnp.int32)
        cond_8 = jax.random.uniform(jax.random.fold_in(_rk, 11), (128, 8), jnp.float32, 0.0, 0.983423)
        return (x, cond_8)
    x, cond_8 = _rec_inputs()

    def _L0_cond_setup():
        import jax, jax.numpy as jnp
        import numpy as np
        B, S, D = (16, 1024, 512)
        E, H = (8, 1024)
        key = jax.random.key(seed)
        ks = jax.random.split(key, 8)
        scale = 0.02
        x = jax.random.normal(ks[0], (B, S, D), dtype=jnp.float32)
        opcode_onehot = jax.random.uniform(ks[1], (B, E), dtype=jnp.float32)
        W_up = jax.random.normal(ks[2], (E, H, D), dtype=jnp.float32) * scale
        b_up = jnp.zeros((E, H), dtype=jnp.float32)
        W_gate = jax.random.normal(ks[3], (E, H, D), dtype=jnp.float32) * scale
        b_gate = jnp.zeros((E, H), dtype=jnp.float32)
        W_down = jax.random.normal(ks[4], (E, D, H), dtype=jnp.float32) * scale
        b_down = jnp.zeros((E, D), dtype=jnp.float32)
        return {'x': x, 'opcode_onehot': opcode_onehot, 'W_up': W_up, 'b_up': b_up, 'W_gate': W_gate, 'b_gate': b_gate, 'W_down': W_down, 'b_down': b_down}
    _L0_cond_all = _L0_cond_setup()
    _L0_cond_in = {k: v for k, v in _L0_cond_all.items() if k in ('W_up', 'b_up', 'W_gate', 'b_gate', 'W_down', 'b_down')}
    del _L0_cond_all

    def _L1_cond_setup():
        import jax, jax.numpy as jnp
        import numpy as np
        R = 16
        ALPHA = 32.0
        SCALING = ALPHA / R
        key = jax.random.key(seed)
        ks = jax.random.split(key, 6)
        B, T, C, O, E = (16, 750, 512, 512, 8)
        x = jax.random.normal(ks[0], (B, T, C), dtype=jnp.float32)
        w = jax.random.uniform(ks[1], (B, E), dtype=jnp.float32)
        W_base = jax.random.normal(ks[2], (O, C), dtype=jnp.float32) * 0.02
        b_base = jax.random.normal(ks[3], (O,), dtype=jnp.float32) * 0.02
        As = jax.random.normal(ks[4], (E, R, C), dtype=jnp.float32) * 0.02
        Bs = jax.random.normal(ks[5], (E, O, R), dtype=jnp.float32) * 0.02
        return {'x': x, 'w': w, 'W_base': W_base, 'b_base': b_base, 'As': As, 'Bs': Bs}
    _L1_cond_all = _L1_cond_setup()
    _L1_cond_in = {k: v for k, v in _L1_cond_all.items() if k in ('W_base', 'b_base', 'As', 'Bs')}
    del _L1_cond_all
    return {'x': x, 'cond_8': cond_8, 'L0_cond_W_up': _L0_cond_in['W_up'], 'L0_cond_b_up': _L0_cond_in['b_up'], 'L0_cond_W_gate': _L0_cond_in['W_gate'], 'L0_cond_b_gate': _L0_cond_in['b_gate'], 'L0_cond_W_down': _L0_cond_in['W_down'], 'L0_cond_b_down': _L0_cond_in['b_down'], 'L1_cond_W_base': _L1_cond_in['W_base'], 'L1_cond_b_base': _L1_cond_in['b_base'], 'L1_cond_As': _L1_cond_in['As'], 'L1_cond_Bs': _L1_cond_in['Bs']}

def reference(x, cond_8, L0_cond_W_up, L0_cond_b_up, L0_cond_W_gate, L0_cond_b_gate, L0_cond_W_down, L0_cond_b_down, L1_cond_W_base, L1_cond_b_base, L1_cond_As, L1_cond_Bs):
    import jax
    import jax.numpy as jnp

    def _L0_cond_ref(x, opcode_onehot, W_up, b_up, W_gate, b_gate, W_down, b_down):
        import jax, jax.numpy as jnp
        import numpy as np
        B, S, D = (16, 1024, 512)
        E, H = (8, 1024)
        expert = jnp.argmax(opcode_onehot, axis=-1)
        wu, bu = (W_up[expert], b_up[expert])
        wg, bg = (W_gate[expert], b_gate[expert])
        wd, bd = (W_down[expert], b_down[expert])
        up = jnp.einsum('bsd,bhd->bsh', x, wu) + bu[:, None, :]
        gate = jnp.einsum('bsd,bhd->bsh', x, wg) + bg[:, None, :]
        hidden = jax.nn.silu(up) * gate
        out = jnp.einsum('bsh,bdh->bsd', hidden, wd) + bd[:, None, :]
        return out

    def _L1_cond_ref(x, w, W_base, b_base, As, Bs):
        import jax, jax.numpy as jnp
        import numpy as np
        R = 16
        ALPHA = 32.0
        SCALING = ALPHA / R
        out = jnp.einsum('btc,oc->bto', x, W_base) + b_base
        h = jnp.einsum('btc,erc->bter', x, As)
        lora = jnp.einsum('bter,eor,be->bto', h, Bs, w)
        return out + lora * SCALING
    x = x + _L0_cond_ref(x, cond_8, L0_cond_W_up, L0_cond_b_up, L0_cond_W_gate, L0_cond_b_gate, L0_cond_W_down, L0_cond_b_down)
    x = x + _L1_cond_ref(x, cond_8, L1_cond_W_base, L1_cond_b_base, L1_cond_As, L1_cond_Bs)
    return x

_drawn_inputs = setup_inputs


def setup_inputs(seed=0):
    import zlib

    import numpy as np

    out = dict(_drawn_inputs(seed))
    spreads = {'L0_cond_b_up': (0.0, 0.499), 'L0_cond_b_gate': (0.0, 0.512), 'L0_cond_b_down': (0.0, 0.1)}
    factors = {'L1_cond_b_base': 3.349}
    for name, (base, spread) in spreads.items():
        noise = np.random.default_rng([zlib.crc32(name.encode()), seed]).standard_normal(out[name].shape)
        drawn = base * np.exp(spread * noise) if base else spread * noise
        out[name] = jnp.asarray(drawn.astype(out[name].dtype))
    for name, factor in factors.items():
        out[name] = (out[name] * factor).astype(out[name].dtype)
    return out
```

```python
from contextlib import ExitStack

import numpy as np

import concourse.bass as bass
from concourse import mybir

ALU = mybir.AluOpType
ACT = mybir.ActivationFunctionType
AX_X = mybir.AxisListType.X
F32 = mybir.dt.float32
F32R = mybir.dt.float32r
I32 = mybir.dt.int32

P = 128
B, S, D = 128, 128, 512
E, H = 8, 1024
R = 16
DC = D // P
NJ = H // P
G = 4
N = G * S
SCALING = 32.0 / R

UP, GATE, DOWN, BIAS = 0, D, 2 * D, 3 * D
NBIAS = 2 + DC
SLICE = 3 * D + NBIAS
XROW = D + 1

MAXT = (B + (G - 1) * E) // G
TILES = MAXT + 2
SLOTS = TILES * G
RING = 4
AHEAD = RING - 1
LOAD = AHEAD + 2
PAD = B

T_LAST, T_EXPERT, T_SLOT = 0, 8, 64
TABLE = T_SLOT + SLOTS

C_TRI = 0
C_ONES = C_TRI + P
C_IDENT = C_ONES + P
C_SLOT = C_IDENT + P
C_FOUR = C_SLOT + SLOTS
C_LT = C_FOUR + E * (B // G)
C_TILE = C_LT + E * E
C_PRIO = C_TILE + TILES * E
C_BATCH = C_PRIO + E
C_ODD = C_BATCH + 1
NCONST = C_ODD + SLOTS

L_BASE, L_A, L_B, L_BIAS = 0, DC * D, DC * D + DC * P, DC * D + DC * P + D
L_MATS = L_BIAS
NL1 = L_BIAS + D


def constants():
    c = np.zeros((P, NCONST), np.float32)
    c[:, C_TRI:C_TRI + P] = np.arange(P)[:, None] < np.arange(P)[None, :]
    c[:, C_ONES:C_ONES + P] = 1.0
    c[:, C_IDENT:C_IDENT + P] = np.eye(P)
    c[:, C_SLOT:C_SLOT + SLOTS] = np.arange(SLOTS)
    c[:, C_FOUR:C_LT] = np.tile(G * np.arange(B // G), E)
    c[:, C_LT:C_TILE] = (np.arange(E)[None, :] < np.arange(E)[:, None]).ravel()
    c[:, C_TILE:C_PRIO] = np.repeat(np.arange(TILES), E)
    c[:, C_PRIO:C_BATCH] = E - np.arange(E)
    c[:, C_BATCH] = np.arange(B) - PAD
    c[:, C_ODD:] = np.arange(SLOTS) % 2
    return c


def build(nc, xt, we, cond, l1, consts, out):
    with ExitStack() as ctx:
        def sb(name, shape, dt=F32):
            return ctx.enter_context(nc.sbuf_tensor(name, shape, dt))

        def bank(name):
            return ctx.enter_context(nc.psum_tensor(name, [P, N], F32))

        def sem(name):
            return ctx.enter_context(nc.semaphore(name))

        w_hi = sb("w_hi", [P, RING, 3 * D], F32R)
        w_lo = sb("w_lo", [P, RING, 3 * D], F32R)
        w_raw = sb("w_raw", [P, 2, SLICE])
        w_bias = sb("w_bias", [P, RING, NBIAS])
        l1_raw = sb("l1_raw", [P, NL1])
        l1_hi = sb("l1_hi", [P, L_MATS], F32R)
        l1_lo = sb("l1_lo", [P, L_MATS], F32R)
        x_raw = sb("x_raw", [P, 2, G, XROW])
        x_hi = sb("x_hi", [P, DC, N], F32R)
        x_lo = sb("x_lo", [P, DC, N], F32R)
        silu = sb("silu", [P, 2, N])
        hid = sb("hid", [P, 2, N])
        hid_hi = sb("hid_hi", [P, 2, N], F32R)
        hid_lo = sb("hid_lo", [P, 2, N], F32R)
        y = sb("y", [P, DC, N])
        y_hi = sb("y_hi", [P, DC, N], F32R)
        y_lo = sb("y_lo", [P, DC, N], F32R)
        a = sb("a", [P, N])
        a_hi = sb("a_hi", [P, N], F32R)
        a_lo = sb("a_lo", [P, N], F32R)
        o_sb = sb("o_sb", [P, 2, D])
        con = sb("con", [P, NCONST])
        cond_sb = sb("cond_sb", [P, E])
        r8 = sb("r8", [P, 8, E])
        r1 = sb("r1", [P, 4])
        table = sb("table", [1, TABLE], I32)
        wide = hid[:, :, :].rearrange("p a n -> p (a n)")

        up_ps, gate_ps, a_ps, o_ps = bank("up_ps"), bank("gate_ps"), bank("a_ps"), bank("o_ps")
        y_ps = [bank(f"y_ps{d}") for d in range(DC)]

        const_in, l1_in = sem("const_in"), sem("l1_in")
        routing, onehot_ok, ranks_ok, places_ok = sem("routing"), sem("onehot_ok"), sem("ranks_ok"), sem("places_ok")
        slots_ok, table_ok = sem("slots_ok"), sem("table_ok")
        l1_sum, l1_hi_ok, l1_ok = sem("l1_sum"), sem("l1_hi_ok"), sem("l1_ok")
        w_in = [sem("w_in0"), sem("w_in1")]
        x_in = sem("x_in")
        w_hi_ok, w_ok = sem("w_hi_ok"), sem("w_ok")
        x_hi_ok, x_ok = sem("x_hi_ok"), sem("x_ok")
        up_ok, gate_ok, down_ok = sem("up_ok"), sem("gate_ok"), sem("down_ok")
        silu_ok, hid_f_ok, hid_hi_ok, hid_ok = sem("silu_ok"), sem("hid_f_ok"), sem("hid_hi_ok"), sem("hid_ok")
        y_f_ok, y_hi_ok, y_ok = sem("y_f_ok"), sem("y_hi_ok"), sem("y_ok")
        a_ps_ok, a_f_ok, a_hi_ok, a_ok = sem("a_ps_ok"), sem("a_f_ok"), sem("a_hi_ok"), sem("a_ok")
        o_ps_ok, o_ok = sem("o_ps_ok"), sem("o_ok")
        stored = [sem("stored0"), sem("stored1")]

        block = ctx.enter_context(nc.Block())

        def last_tile(eng):
            eng.wait_ge(table_ok, 1)
            return eng.value_load(table[0:1, T_LAST:T_LAST + 1], min_val=B // G - 1, max_val=MAXT - 1)

        @block.sync
        def _(sp):
            sp.dma_start(con[:, :], consts).then_inc(const_in, 16)
            sp.dma_start(cond_sb[:, :], cond).then_inc(const_in, 16)
            sp.dma_start(l1_raw[:, :], l1).then_inc(l1_in, 16)
            last = last_tile(sp)

            def expert(t):
                return sp.value_load(table[0:1, bass.ds(T_EXPERT + t, 1)], min_val=0, max_val=E - 1)

            def batches(t):
                return [sp.value_load(table[0:1, bass.ds(T_SLOT + G * t + i, 1)], min_val=0, max_val=PAD + 1)
                        for i in range(G)]

            def load_slice(e, j, n):
                sp.dma_start(w_raw[:, n % 2, :], we[e, j]).then_inc(w_in[n % 2], 16)

            def load_x(t, b):
                for i in range(G):
                    sp.dma_start(x_raw[:, bass.ds(t % 2, 1), i, :], xt[b[i]]).then_inc(x_in, 16)

            def store(t, u, b):
                sp.wait_ge(o_ok, G * t + u + 1)
                sp.wait_ge(table_ok, 1)
                sp.dma_start(out[b[u]], o_sb[:, u % 2, :]).then_inc(stored[u % 2], 16)

            def tile(t, first):
                here, after = expert(t), expert(t + 1)
                ahead = batches(t + 1)
                back = None if first else batches(t - 1)
                for j in range(NJ):
                    sp.wait_ge(w_ok, NJ * t + j + AHEAD + 1)
                    sp.wait_ge(table_ok, 1)
                    n = j + LOAD
                    load_slice(here if n < NJ else after, n % NJ, n)
                    if j == 2:
                        if not first:
                            sp.wait_ge(a_f_ok, t)
                            sp.wait_ge(table_ok, 1)
                        load_x(t + 1, ahead)
                    if not first and 3 <= j < 3 + G:
                        store(t - 1, j - 3, back)

            e0 = expert(0)
            load_slice(e0, 0, 0)
            load_x(0, batches(0))
            load_slice(e0, 1, 1)
            for n in range(2, LOAD):
                sp.wait_ge(w_ok, n - 1)
                load_slice(e0, n, n)
            tile(0, True)
            with sp.Fori(1, last + 1) as t:
                tile(t, False)
            back = batches(last)
            for u in range(G):
                store(last, u, back)
        @block.gpsimd
        def _(pool):
            last = last_tile(pool)
            for k in range(2):
                pool.wait_ge(stored[k], 16 * (G // 2) * (last + 1))

        @block.tensor
        def _(pe):
            pe.wait_ge(onehot_ok, 1)
            nc.tensor.matmul(a_ps[:, 0:E], con[:, C_TRI:C_TRI + P], r8[:, 1, :], start=True, stop=True)
            nc.tensor.matmul(o_ps[:, 0:E], con[:, C_ONES:C_ONES + P], r8[:, 1, :], start=True,
                             stop=True).then_inc(ranks_ok, 1)
            pe.wait_ge(places_ok, 1)
            nc.tensor.matmul(up_ps[0:1, 0:SLOTS], con[:, C_BATCH:C_BATCH + 1], wide[:, 0:SLOTS], start=True,
                             stop=True).then_inc(slots_ok, 1)
            last = last_tile(pe)

            def product(ps, left_hi, left_lo, right_hi, right_lo, start, stop):
                nc.tensor.matmul(ps, left_hi, right_hi, start=start, stop=False)
                nc.tensor.matmul(ps, left_hi, right_lo, start=False, stop=False)
                return nc.tensor.matmul(ps, left_lo, right_hi, start=False, stop=stop)

            def up_or_gate(ps, t, j, at, done):
                k = j % RING
                for c in range(DC):
                    if at == UP and j == 0:
                        pe.wait_ge(x_ok, DC * t + c + 1)
                    w = slice(at + c * P, at + (c + 1) * P)
                    ins = product(ps[:, :], w_hi[:, k, w], w_lo[:, k, w], x_hi[:, c, :], x_lo[:, c, :],
                                   c == 0, c == DC - 1)
                ins.then_inc(done, 1)

            def down(t, j):
                pe.wait_ge(hid_ok, NJ * t + j + 1)
                if j == 0:
                    pe.wait_ge(y_f_ok, DC * t)
                k = j % RING
                for d in range(DC):
                    w = slice(DOWN + d * P, DOWN + (d + 1) * P)
                    ins = product(y_ps[d][:, :], w_hi[:, k, w], w_lo[:, k, w], hid_hi[:, j % 2, :],
                                   hid_lo[:, j % 2, :], j == 0, j == NJ - 1)
                ins.then_inc(down_ok, 1)

            def lora_a(t):
                pe.wait_ge(l1_ok, 1)
                pe.wait_ge(a_f_ok, t)
                for c in range(DC):
                    pe.wait_ge(y_ok, DC * t + c + 1)
                    w = slice(L_A + c * P, L_A + (c + 1) * P)
                    ins = product(a_ps[:, :], l1_hi[:, w], l1_lo[:, w], y_hi[:, c, :], y_lo[:, c, :],
                                   c == 0, c == DC - 1)
                ins.then_inc(a_ps_ok, 1)

            def outputs(t, u):
                pe.wait_ge(o_ok, G * t + u)
                rows = slice(u * S, (u + 1) * S)
                for c in range(DC):
                    w = slice(L_BASE + c * D, L_BASE + (c + 1) * D)
                    product(o_ps[:, :], y_hi[:, c, rows], y_lo[:, c, rows], l1_hi[:, w], l1_lo[:, w],
                            c == 0, False)
                pe.wait_ge(a_ok, t + 1)
                w = slice(L_B, L_B + D)
                product(o_ps[:, :], a_hi[:, rows], a_lo[:, rows], l1_hi[:, w], l1_lo[:, w],
                        False, True).then_inc(o_ps_ok, 1)

            def tile(t, first):
                for j in range(NJ):
                    pe.wait_ge(w_ok, NJ * t + j + 1)
                    pe.wait_ge(silu_ok, NJ * t + j)
                    up_or_gate(up_ps, t, j, UP, up_ok)
                    pe.wait_ge(hid_f_ok, NJ * t + j)
                    up_or_gate(gate_ps, t, j, GATE, gate_ok)
                    if j >= 1:
                        down(t, j - 1)
                    if not first and j == 1:
                        lora_a(t - 1)
                    if not first and 2 <= j < 2 + G:
                        outputs(t - 1, j - 2)
                down(t, NJ - 1)

            tile(0, True)
            with pe.Fori(1, last + 1) as t:
                tile(t, False)
            lora_a(last)
            for u in range(G):
                outputs(last, u)

        @block.scalar
        def _(act):
            act.wait_ge(l1_sum, 1)
            nc.scalar.activation(l1_hi[:, :], l1_raw[:, 0:L_MATS], ACT.Copy).then_inc(l1_hi_ok, 1)
            last = last_tile(act)

            def split_slice(n, freed):
                if freed is not None:
                    act.wait_ge(down_ok, freed)
                nc.scalar.activation(w_hi[:, n % RING, :], w_raw[:, n % 2, 0:BIAS], ACT.Copy).then_inc(w_hi_ok, 1)

            def split_x(t, c):
                nc.scalar.activation(x_hi[:, c, :].rearrange("p (g s) -> p g s", g=G),
                                     x_raw[:, bass.ds(t % 2, 1), :, c * P:(c + 1) * P].rearrange(
                                         "p o g s -> p (o g) s"),
                                     ACT.Copy).then_inc(x_hi_ok, 1)

            def split_a(t):
                act.wait_ge(a_f_ok, t + 1)
                nc.scalar.activation(a_hi[:, :], a[:, :], ACT.Copy).then_inc(a_hi_ok, 1)

            def slice_landed(t, j, ahead):
                n = j + ahead
                return w_in[n % 2], 16 * (NJ // 2) * t + 16 * (n // 2 + 1)

            def tile(t, first):
                for j in range(NJ):
                    s = NJ * t + j
                    act.wait_ge(up_ok, s + 1)
                    nc.scalar.activation(silu[:, j % 2, :], up_ps[:, :], ACT.Silu,
                                         bias=w_bias[:, j % RING, 0:1]).then_inc(silu_ok, 1)
                    if not first and j == 2:
                        split_a(t - 1)
                    if j == NJ - 1:
                        act.wait_ge(x_in, 16 * G * (t + 2))
                        act.wait_ge(gate_ok, s + 1)
                        split_x(t + 1, 0)
                    act.wait_ge(hid_f_ok, s + 1)
                    nc.scalar.activation(hid_hi[:, j % 2, :], hid[:, j % 2, :], ACT.Copy).then_inc(hid_hi_ok, 1)
                    if j == NJ - 1:
                        for c in range(1, DC):
                            split_x(t + 1, c)
                    landed, count = slice_landed(t, j, AHEAD)
                    act.wait_ge(landed, count)
                    split_slice(j + AHEAD, s)
                for d in range(DC):
                    act.wait_ge(y_f_ok, DC * t + d + 1)
                    nc.scalar.activation(y_hi[:, d, :], y[:, d, :], ACT.Copy).then_inc(y_hi_ok, 1)

            for n in range(AHEAD):
                landed, count = slice_landed(0, n, 0)
                act.wait_ge(landed, count)
                split_slice(n, None)
                if n == 0:
                    act.wait_ge(x_in, 16 * G)
                    for c in range(DC):
                        split_x(0, c)
            tile(0, True)
            with act.Fori(1, last + 1) as t:
                tile(t, False)
            for n in range(AHEAD, LOAD):
                landed, count = slice_landed(last, NJ, n)
                act.wait_ge(landed, count)
            split_a(last)

        @block.vector
        def _(dve):
            step = [0]

            def link(ins):
                step[0] += 1
                ins.then_inc(routing, 1)
                dve.wait_ge(routing, step[0])

            onehot, ranks, counts, tiles_of = r8[:, 1, :], r8[:, 2, :], r8[:, 3, :], r8[:, 4, :]
            starts, ends, places = r8[:, 5, :], r8[:, 6, :], r8[:, 7, :]

            dve.wait_ge(const_in, 32)
            link(nc.vector.reduce_max(r1[:, 0:1], cond_sb[:, :], AX_X))
            link(nc.vector.scalar_tensor_tensor(out=r8[:, 0, :], in0=cond_sb[:, :], scalar=r1[:, 0:1],
                                                in1=con[:, C_PRIO:C_PRIO + E], op0=ALU.is_equal, op1=ALU.mult))
            link(nc.vector.reduce_max(r1[:, 1:2], r8[:, 0, :], AX_X))
            nc.vector.tensor_scalar(onehot, r8[:, 0, :], r1[:, 1:2], None, ALU.is_equal).then_inc(onehot_ok, 1)
            dve.wait_ge(ranks_ok, 1)
            nc.vector.tensor_copy(ranks, a_ps[:, 0:E])
            link(nc.vector.tensor_copy(counts, o_ps[:, 0:E]))
            more = wide[:, 0:E * (B // G)].rearrange("p (e k) -> p e k", e=E)
            link(nc.vector.tensor_tensor(
                more, counts.unsqueeze(2).to_broadcast([P, E, B // G]),
                con[:, C_FOUR:C_LT].rearrange("p (e k) -> p e k", e=E), ALU.is_gt))
            link(nc.vector.reduce_sum(tiles_of, more, AX_X))
            below = wide[:, 512:512 + E * E].rearrange("p (e k) -> p e k", e=E)
            link(nc.vector.tensor_tensor(
                below, tiles_of.unsqueeze(1).to_broadcast([P, E, E]),
                con[:, C_LT:C_TILE].rearrange("p (e k) -> p e k", e=E), ALU.mult))
            link(nc.vector.reduce_sum(starts, below, AX_X))
            nc.vector.tensor_tensor(ends, starts, tiles_of, ALU.add)
            link(nc.vector.scalar_tensor_tensor(out=places, in0=starts, scalar=float(G), in1=ranks,
                                                op0=ALU.mult, op1=ALU.add))
            link(nc.vector.tensor_tensor(places, places, onehot, ALU.mult))
            link(nc.vector.reduce_sum(r1[:, 2:3], places, AX_X))
            nc.vector.tensor_scalar(wide[:, 0:SLOTS], con[:, C_SLOT:C_SLOT + SLOTS], r1[:, 2:3], None,
                                    ALU.is_equal).then_inc(places_ok, 1)
            passed = wide[0:1, 512:512 + TILES * E].rearrange("p (t e) -> p t e", e=E)
            link(nc.vector.tensor_tensor(
                passed, con[0:1, C_TILE:C_PRIO].rearrange("p (t e) -> p t e", e=E),
                ends[0:1, :].unsqueeze(1).to_broadcast([1, TILES, E]), ALU.is_ge))
            link(nc.vector.reduce_sum(wide[0:1, 1000 - TILES:1000], passed, AX_X))
            nc.vector.tensor_scalar(table[0:1, T_EXPERT:T_EXPERT + TILES], wide[0:1, 1000 - TILES:1000],
                                    float(E - 1), None, ALU.min)
            nc.vector.tensor_scalar(table[0:1, T_LAST:T_LAST + 1], ends[0:1, E - 1:E], -1.0, None, ALU.add)
            dve.wait_ge(slots_ok, 1)
            link(nc.vector.scalar_tensor_tensor(
                out=wide[0:1, 0:SLOTS], in0=up_ps[0:1, 0:SLOTS], scalar=0.0,
                in1=con[0:1, C_ODD:C_ODD + SLOTS], op0=ALU.is_ge, op1=ALU.mult))
            nc.vector.scalar_tensor_tensor(
                out=table[0:1, T_SLOT:T_SLOT + SLOTS], in0=up_ps[0:1, 0:SLOTS], scalar=float(PAD),
                in1=wide[0:1, 0:SLOTS], op0=ALU.add, op1=ALU.add).then_inc(table_ok, 1)

            dve.wait_ge(l1_in, 16)
            for c in range(DC):
                at = slice(L_BASE + c * D + c * P, L_BASE + c * D + (c + 1) * P)
                ins = nc.vector.tensor_tensor(l1_raw[:, at], l1_raw[:, at], con[:, C_IDENT:C_IDENT + P], ALU.add)
            ins.then_inc(l1_sum, 1)
            dve.wait_ge(l1_hi_ok, 1)
            nc.vector.tensor_tensor(l1_lo[:, :], l1_raw[:, 0:L_MATS], l1_hi[:, :], ALU.subtract).then_inc(l1_ok, 1)
            last = last_tile(dve)

            def split_slice(s_ahead, n):
                dve.wait_ge(w_hi_ok, s_ahead + 1)
                nc.vector.tensor_copy(w_bias[:, n % RING, :], w_raw[:, n % 2, BIAS:SLICE])
                nc.vector.tensor_tensor(w_lo[:, n % RING, :], w_raw[:, n % 2, 0:BIAS], w_hi[:, n % RING, :],
                                        ALU.subtract).then_inc(w_ok, 1)

            def split_x(t, c):
                dve.wait_ge(x_hi_ok, DC * t + c + 1)
                nc.vector.tensor_tensor(x_lo[:, c, :].rearrange("p (g s) -> p g s", g=G),
                                        x_raw[:, bass.ds(t % 2, 1), :, c * P:(c + 1) * P].rearrange(
                                            "p o g s -> p (o g) s"),
                                        x_hi[:, c, :].rearrange("p (g s) -> p g s", g=G),
                                        ALU.subtract).then_inc(x_ok, 1)

            def y_sum(t, d):
                nc.vector.scalar_tensor_tensor(
                    out=y[:, d, :].rearrange("p (g s) -> p g s", g=G),
                    in0=y_ps[d][:, :].rearrange("p (g s) -> p g s", g=G),
                    scalar=w_bias[:, (NJ - 1) % RING, 2 + d:3 + d],
                    in1=x_raw[:, bass.ds(t % 2, 1), :, d * P:(d + 1) * P].rearrange("p o g s -> p (o g) s"),
                    op0=ALU.add, op1=ALU.add).then_inc(y_f_ok, 1)

            def y_low(t, d):
                dve.wait_ge(y_hi_ok, DC * t + d + 1)
                nc.vector.tensor_tensor(y_lo[:, d, :], y[:, d, :], y_hi[:, d, :],
                                        ALU.subtract).then_inc(y_ok, 1)

            def weigh_a(t):
                dve.wait_ge(a_ps_ok, t + 1)
                weight = x_raw[:, bass.ds(t % 2, 1), :, D:XROW].rearrange("p o g s -> p (o g) s")
                nc.vector.scalar_tensor_tensor(
                    out=a[:, :].rearrange("p (g s) -> p g s", g=G),
                    in0=a_ps[:, :].rearrange("p (g s) -> p g s", g=G), scalar=SCALING,
                    in1=weight.to_broadcast([P, G, S]), op0=ALU.mult, op1=ALU.mult).then_inc(a_f_ok, 1)

            def split_a(t):
                dve.wait_ge(a_hi_ok, t + 1)
                nc.vector.tensor_tensor(a_lo[:, :], a[:, :], a_hi[:, :], ALU.subtract).then_inc(a_ok, 1)

            def drain_output(t, u):
                dve.wait_ge(o_ps_ok, G * t + u + 1)
                dve.wait_ge(stored[u % 2], 16 * (G // 2) * t + 16 * (u // 2))
                nc.vector.tensor_tensor(o_sb[:, u % 2, :], o_ps[:, :], l1_raw[:, L_BIAS:NL1],
                                        ALU.add).then_inc(o_ok, 1)

            def tile(t, first):
                for j in range(NJ):
                    s = NJ * t + j
                    if not first and j == 2:
                        weigh_a(t - 1)
                        split_a(t - 1)
                    if not first and 3 <= j < 3 + G:
                        drain_output(t - 1, j - 3)
                    dve.wait_ge(gate_ok, s + 1)
                    dve.wait_ge(silu_ok, s + 1)
                    nc.vector.scalar_tensor_tensor(out=hid[:, j % 2, :], in0=gate_ps[:, :],
                                                   scalar=w_bias[:, j % RING, 1:2], in1=silu[:, j % 2, :],
                                                   op0=ALU.add, op1=ALU.mult).then_inc(hid_f_ok, 1)
                    if j == NJ - 1:
                        split_x(t + 1, 0)
                    dve.wait_ge(hid_hi_ok, s + 1)
                    nc.vector.tensor_tensor(hid_lo[:, j % 2, :], hid[:, j % 2, :], hid_hi[:, j % 2, :],
                                            ALU.subtract).then_inc(hid_ok, 1)
                    if j == NJ - 1:
                        for c in range(1, DC):
                            split_x(t + 1, c)
                    if (j + AHEAD) % RING == (NJ - 1) % RING:
                        dve.wait_ge(y_f_ok, DC * t)
                    split_slice(s + AHEAD, j + AHEAD)
                dve.wait_ge(down_ok, NJ * (t + 1))
                dve.wait_ge(y_ok, DC * t)
                for d in range(DC):
                    y_sum(t, d)
                for d in range(DC):
                    y_low(t, d)

            for n in range(AHEAD):
                split_slice(n, n)
                if n == 0:
                    for c in range(DC):
                        split_x(0, c)
            tile(0, True)
            with dve.Fori(1, last + 1) as t:
                tile(t, False)
            weigh_a(last)
            split_a(last)
            for u in range(G):
                drain_output(last, u)


def lay_out(x, cond_8, W_up, b_up, W_gate, b_gate, W_down, b_down, W_base, b_base, As, Bs):
    xt = np.zeros((B + 2, P, XROW), np.float32)
    xt[:B, :, :D] = x.reshape(B, S, DC, P).transpose(0, 3, 2, 1).reshape(B, P, D)
    xt[:B, :, D] = np.repeat(cond_8, R, axis=1)
    we = np.empty((E, NJ, P, SLICE), np.float32)
    for at, w in ((UP, W_up), (GATE, W_gate)):
        we[..., at:at + D] = w.reshape(E, NJ, P, DC, P).transpose(0, 1, 4, 3, 2).reshape(E, NJ, P, D)
    we[..., DOWN:BIAS] = W_down.reshape(E, D, NJ, P).transpose(0, 2, 3, 1)
    we[..., BIAS] = b_up.reshape(E, NJ, P)
    we[..., BIAS + 1] = b_gate.reshape(E, NJ, P)
    we[..., BIAS + 2:] = b_down.reshape(E, 1, DC, P).transpose(0, 1, 3, 2)
    l1 = np.empty((P, NL1), np.float32)
    l1[:, L_BASE:L_A] = W_base.reshape(D, DC, P).transpose(2, 1, 0).reshape(P, DC * D)
    l1[:, L_A:L_B] = As.reshape(E * R, DC, P).transpose(2, 1, 0).reshape(P, DC * P)
    l1[:, L_B:L_BIAS] = Bs.transpose(0, 2, 1).reshape(E * R, D)
    l1[:, L_BIAS:] = b_base[None, :]
    return {"xt": xt, "we": we, "cond": np.ascontiguousarray(cond_8), "l1": l1, "consts": constants()}


def kernel(x, cond_8, L0_cond_W_up, L0_cond_b_up, L0_cond_W_gate, L0_cond_b_gate, L0_cond_W_down,
           L0_cond_b_down, L1_cond_W_base, L1_cond_b_base, L1_cond_As, L1_cond_Bs):
    import concourse.bacc as bacc
    from concourse.bass_utils import run_bass_kernel_spmd

    arrays = lay_out(*(np.asarray(v) for v in (
        x, cond_8, L0_cond_W_up, L0_cond_b_up, L0_cond_W_gate, L0_cond_b_gate, L0_cond_W_down,
        L0_cond_b_down, L1_cond_W_base, L1_cond_b_base, L1_cond_As, L1_cond_Bs)))
    nc = bacc.Bacc("TRN2", target_bir_lowering=False, num_devices=1)
    aps = [nc.dram_tensor(k, v.shape, F32, kind="ExternalInput").ap() for k, v in arrays.items()]
    out = nc.dram_tensor("out", (B + 2, S, D), F32, kind="ExternalOutput").ap()
    build(nc, *aps, out)
    got = run_bass_kernel_spmd(nc, [arrays], core_ids=[0])
    return got.results[0]["out"][:B]
```

```python
from contextlib import ExitStack

import numpy as np

import concourse.bass as bass
from concourse import mybir

ALU = mybir.AluOpType
ACT = mybir.ActivationFunctionType
AX_X = mybir.AxisListType.X
F32 = mybir.dt.float32
F32R = mybir.dt.float32r
I32 = mybir.dt.int32

P = 128
B, S, D = 128, 128, 512
E, H = 8, 1024
R = 16
DC = D // P
NJ = H // P
G = 4
HALF = G // 2
N = G * S
SCALING = 32.0 / R

UP, GATE, DOWN, BIAS = 0, D, 2 * D, 3 * D
NBIAS = 2 + DC
SLICE = 3 * D + NBIAS
XROW = D + 1

MIN_WHOLE = (B - HALF * E) // G
MAXT = (B + (G - 1) * E) // G
MIN_HALVES = 2
TILES = MAXT + 2
SLOTS = TILES * G
RING = 4
AHEAD = RING - 1
LOAD = AHEAD + 2
PAD = B

T_WHOLE, T_LAST, T_EXPERT, T_SLOT = 0, 1, 8, 64
TABLE = T_SLOT + SLOTS

C_TRI = 0
C_ONES = C_TRI + P
C_IDENT = C_ONES + P
C_SLOT = C_IDENT + P
C_FOUR = C_SLOT + SLOTS
C_LT = C_FOUR + E * (B // G)
C_TILE = C_LT + 4 * E * E
C_PRIO = C_TILE + TILES * 2 * E
C_BATCH = C_PRIO + E
C_ODD = C_BATCH + 1
NCONST = C_ODD + SLOTS

L_BASE, L_A, L_B, L_BIAS = 0, DC * D, DC * D + DC * P, DC * D + DC * P + D
L_MATS = L_BIAS
NL1 = L_BIAS + D


def constants():
    c = np.zeros((P, NCONST), np.float32)
    c[:, C_TRI:C_TRI + P] = np.arange(P)[:, None] < np.arange(P)[None, :]
    c[:, C_ONES:C_ONES + P] = 1.0
    c[:, C_IDENT:C_IDENT + P] = np.eye(P)
    c[:, C_SLOT:C_SLOT + SLOTS] = np.arange(SLOTS)
    c[:, C_FOUR:C_LT] = np.tile(G * np.arange(B // G) + HALF, E)
    c[:, C_LT:C_TILE] = (np.arange(2 * E)[None, :] < np.arange(2 * E)[:, None]).ravel()
    c[:, C_TILE:C_PRIO] = np.repeat(np.arange(TILES), 2 * E)
    c[:, C_PRIO:C_BATCH] = E - np.arange(E)
    c[:, C_BATCH] = np.arange(B) - PAD
    c[:, C_ODD:] = np.arange(SLOTS) % 2
    return c


def build(nc, xt, we, cond, l1, consts, out):
    with ExitStack() as ctx:
        def sb(name, shape, dt=F32):
            return ctx.enter_context(nc.sbuf_tensor(name, shape, dt))

        def bank(name):
            return ctx.enter_context(nc.psum_tensor(name, [P, N], F32))

        def sem(name):
            return ctx.enter_context(nc.semaphore(name))

        w_hi = sb("w_hi", [P, RING, 3 * D], F32R)
        w_lo = sb("w_lo", [P, RING, 3 * D], F32R)
        w_raw = sb("w_raw", [P, 2, SLICE])
        w_bias = sb("w_bias", [P, RING, NBIAS])
        l1_raw = sb("l1_raw", [P, NL1])
        l1_hi = sb("l1_hi", [P, L_MATS], F32R)
        l1_lo = sb("l1_lo", [P, L_MATS], F32R)
        x_raw = sb("x_raw", [P, 2, G, XROW])
        x_hi = sb("x_hi", [P, DC, N], F32R)
        x_lo = sb("x_lo", [P, DC, N], F32R)
        silu = sb("silu", [P, 2, N])
        hid = sb("hid", [P, 2, N])
        hid_hi = sb("hid_hi", [P, 2, N], F32R)
        hid_lo = sb("hid_lo", [P, 2, N], F32R)
        y = sb("y", [P, DC, N])
        y_hi = sb("y_hi", [P, DC, N], F32R)
        y_lo = sb("y_lo", [P, DC, N], F32R)
        a = sb("a", [P, N])
        a_hi = sb("a_hi", [P, N], F32R)
        a_lo = sb("a_lo", [P, N], F32R)
        o_sb = sb("o_sb", [P, 2, D])
        con = sb("con", [P, NCONST])
        cond_sb = sb("cond_sb", [P, E])
        r8 = sb("r8", [P, 6, E])
        r16 = sb("r16", [P, 3, 2 * E])
        r1 = sb("r1", [P, 4])
        table = sb("table", [1, TABLE], I32)
        wide = x_raw[:, :, :, :].rearrange("p a g n -> p (a g n)")

        up_ps, gate_ps, a_ps, o_ps = bank("up_ps"), bank("gate_ps"), bank("a_ps"), bank("o_ps")
        y_ps = [bank(f"y_ps{d}") for d in range(DC)]

        const_in, l1_in = sem("const_in"), sem("l1_in")
        routing, onehot_ok, ranks_ok, places_ok = sem("routing"), sem("onehot_ok"), sem("ranks_ok"), sem("places_ok")
        slots_ok, table_ok = sem("slots_ok"), sem("table_ok")
        l1_sum, l1_hi_ok, l1_ok = sem("l1_sum"), sem("l1_hi_ok"), sem("l1_ok")
        w_in = [sem("w_in0"), sem("w_in1")]
        x_in = sem("x_in")
        w_hi_ok, w_ok = sem("w_hi_ok"), sem("w_ok")
        x_hi_ok, x_ok = sem("x_hi_ok"), sem("x_ok")
        up_ok, gate_ok, down_ok = sem("up_ok"), sem("gate_ok"), sem("down_ok")
        silu_ok, hid_f_ok, hid_hi_ok, hid_ok = sem("silu_ok"), sem("hid_f_ok"), sem("hid_hi_ok"), sem("hid_ok")
        y_f_ok, y_hi_ok, y_ok = sem("y_f_ok"), sem("y_hi_ok"), sem("y_ok")
        a_ps_ok, a_f_ok, a_hi_ok, a_ok = sem("a_ps_ok"), sem("a_f_ok"), sem("a_hi_ok"), sem("a_ok")
        o_ps_ok, o_ok = sem("o_ps_ok"), sem("o_ok")
        stored = [sem("stored0"), sem("stored1")]

        block = ctx.enter_context(nc.Block())

        def last_tiles(eng):
            eng.wait_ge(table_ok, 1)
            return (eng.value_load(table[0:1, T_WHOLE:T_WHOLE + 1], min_val=MIN_WHOLE - 1, max_val=B // G - 1),
                    eng.value_load(table[0:1, T_LAST:T_LAST + 1], min_val=MIN_WHOLE + 1, max_val=MAXT - 1))

        def whole_units(t):
            return G * t

        def half_units(t, whole):
            return HALF * t + HALF * (whole + 1)

        def run(eng, whole, last, tile, finish):
            tile(0, G, None)
            with eng.Fori(1, whole + 1) as t:
                tile(t, G, (t - 1, G, whole_units(t - 1)))
            tile(whole + 1, HALF, (whole, G, whole_units(whole)))
            with eng.Fori(whole + 2, last + 1) as t:
                tile(t, HALF, (t - 1, HALF, half_units(t - 1, whole)))
            finish(last, HALF, half_units(last, whole))

        @block.sync
        def _(sp):
            sp.dma_start(con[:, :], consts).then_inc(const_in, 16)
            sp.dma_start(cond_sb[:, :], cond).then_inc(const_in, 16)
            sp.dma_start(l1_raw[:, :], l1).then_inc(l1_in, 16)
            whole, last = last_tiles(sp)

            def expert(t):
                return sp.value_load(table[0:1, bass.ds(T_EXPERT + t, 1)], min_val=0, max_val=E - 1)

            def batches(t, n):
                return [sp.value_load(table[0:1, bass.ds(T_SLOT + G * t + i, 1)], min_val=0, max_val=PAD + 1)
                        for i in range(n)]

            def load_slice(e, j, n):
                sp.dma_start(w_raw[:, n % 2, :], we[e, j]).then_inc(w_in[n % 2], 16)

            def load_x(t, b):
                for i in range(G):
                    sp.dma_start(x_raw[:, bass.ds(t % 2, 1), i, :], xt[b[i]]).then_inc(x_in, 16)

            def store(unit0, u, b):
                sp.wait_ge(o_ok, unit0 + u + 1)
                sp.wait_ge(table_ok, 1)
                sp.dma_start(out[b[u]], o_sb[:, u % 2, :]).then_inc(stored[u % 2], 16)

            def tile(t, n, back):
                here, after = expert(t), expert(t + 1)
                ahead = batches(t + 1, G)
                if back is not None:
                    back_t, back_n, unit0 = back
                    back_b = batches(back_t, back_n)
                for j in range(NJ):
                    sp.wait_ge(w_ok, NJ * t + j + AHEAD + 1)
                    sp.wait_ge(table_ok, 1)
                    k = j + LOAD
                    load_slice(here if k < NJ else after, k % NJ, k)
                    if j == 2:
                        if back is not None:
                            sp.wait_ge(a_f_ok, t)
                            sp.wait_ge(table_ok, 1)
                        load_x(t + 1, ahead)
                    if back is not None and 3 <= j < 3 + back_n:
                        store(unit0, j - 3, back_b)

            def finish(t, n, unit0):
                b = batches(t, n)
                for u in range(n):
                    store(unit0, u, b)

            e0 = expert(0)
            load_slice(e0, 0, 0)
            load_x(0, batches(0, G))
            load_slice(e0, 1, 1)
            for n in range(2, LOAD):
                sp.wait_ge(w_ok, n - 1)
                load_slice(e0, n, n)
            run(sp, whole, last, tile, finish)

        @block.gpsimd
        def _(pool):
            whole, last = last_tiles(pool)
            for k in range(2):
                pool.wait_ge(stored[k], 16 * (last + 1 + whole + 1))

        @block.tensor
        def _(pe):
            pe.wait_ge(onehot_ok, 1)
            nc.tensor.matmul(a_ps[:, 0:E], con[:, C_TRI:C_TRI + P], r8[:, 1, :], start=True, stop=True)
            nc.tensor.matmul(o_ps[:, 0:E], con[:, C_ONES:C_ONES + P], r8[:, 1, :], start=True,
                             stop=True).then_inc(ranks_ok, 1)
            pe.wait_ge(places_ok, 1)
            nc.tensor.matmul(up_ps[0:1, 0:SLOTS], con[:, C_BATCH:C_BATCH + 1], wide[:, 0:SLOTS], start=True,
                             stop=True).then_inc(slots_ok, 1)
            whole, last = last_tiles(pe)

            def product(ps, left_hi, left_lo, right_hi, right_lo, start, stop):
                nc.tensor.matmul(ps, left_hi, right_hi, start=start, stop=False)
                nc.tensor.matmul(ps, left_hi, right_lo, start=False, stop=False)
                return nc.tensor.matmul(ps, left_lo, right_hi, start=False, stop=stop)

            def up_or_gate(ps, t, n, j, at, done):
                k = j % RING
                for c in range(DC):
                    if at == UP and j == 0:
                        pe.wait_ge(x_ok, DC * t + c + 1)
                    w = slice(at + c * P, at + (c + 1) * P)
                    ins = product(ps[:, 0:n * S], w_hi[:, k, w], w_lo[:, k, w], x_hi[:, c, 0:n * S], x_lo[:, c, 0:n * S],
                                   c == 0, c == DC - 1)
                ins.then_inc(done, 1)

            def down(t, n, j):
                pe.wait_ge(hid_ok, NJ * t + j + 1)
                if j == 0:
                    pe.wait_ge(y_f_ok, DC * t)
                k = j % RING
                for d in range(DC):
                    w = slice(DOWN + d * P, DOWN + (d + 1) * P)
                    ins = product(y_ps[d][:, 0:n * S], w_hi[:, k, w], w_lo[:, k, w], hid_hi[:, j % 2, 0:n * S],
                                   hid_lo[:, j % 2, 0:n * S], j == 0, j == NJ - 1)
                ins.then_inc(down_ok, 1)

            def lora_a(t, n):
                pe.wait_ge(l1_ok, 1)
                pe.wait_ge(a_f_ok, t)
                for c in range(DC):
                    pe.wait_ge(y_ok, DC * t + c + 1)
                    w = slice(L_A + c * P, L_A + (c + 1) * P)
                    ins = product(a_ps[:, 0:n * S], l1_hi[:, w], l1_lo[:, w], y_hi[:, c, 0:n * S], y_lo[:, c, 0:n * S],
                                   c == 0, c == DC - 1)
                ins.then_inc(a_ps_ok, 1)

            def outputs(t, unit0, u):
                pe.wait_ge(o_ok, unit0 + u)
                rows = slice(u * S, (u + 1) * S)
                for c in range(DC):
                    w = slice(L_BASE + c * D, L_BASE + (c + 1) * D)
                    product(o_ps[:, :], y_hi[:, c, rows], y_lo[:, c, rows], l1_hi[:, w], l1_lo[:, w],
                            c == 0, False)
                pe.wait_ge(a_ok, t + 1)
                w = slice(L_B, L_B + D)
                product(o_ps[:, :], a_hi[:, rows], a_lo[:, rows], l1_hi[:, w], l1_lo[:, w],
                        False, True).then_inc(o_ps_ok, 1)

            def tile(t, n, back):
                if back is not None:
                    back_t, back_n, unit0 = back
                for j in range(NJ):
                    pe.wait_ge(w_ok, NJ * t + j + 1)
                    pe.wait_ge(silu_ok, NJ * t + j)
                    up_or_gate(up_ps, t, n, j, UP, up_ok)
                    pe.wait_ge(hid_f_ok, NJ * t + j)
                    up_or_gate(gate_ps, t, n, j, GATE, gate_ok)
                    if j >= 1:
                        down(t, n, j - 1)
                    if back is not None and j == 1:
                        lora_a(back_t, back_n)
                    if back is not None and 2 <= j < 2 + back_n:
                        outputs(back_t, unit0, j - 2)
                down(t, n, NJ - 1)

            def finish(t, n, unit0):
                lora_a(t, n)
                for u in range(n):
                    outputs(t, unit0, u)

            run(pe, whole, last, tile, finish)

        @block.scalar
        def _(act):
            act.wait_ge(l1_sum, 1)
            nc.scalar.activation(l1_hi[:, :], l1_raw[:, 0:L_MATS], ACT.Copy).then_inc(l1_hi_ok, 1)
            whole, last = last_tiles(act)

            def split_slice(n, freed):
                if freed is not None:
                    act.wait_ge(down_ok, freed)
                nc.scalar.activation(w_hi[:, n % RING, :], w_raw[:, n % 2, 0:BIAS], ACT.Copy).then_inc(w_hi_ok, 1)

            def split_x(t, n, c):
                nc.scalar.activation(x_hi[:, c, 0:n * S].rearrange("p (g s) -> p g s", g=n),
                                     x_raw[:, bass.ds(t % 2, 1), 0:n, c * P:(c + 1) * P].rearrange(
                                         "p o g s -> p (o g) s"),
                                     ACT.Copy).then_inc(x_hi_ok, 1)

            def split_a(t, n):
                act.wait_ge(a_f_ok, t + 1)
                nc.scalar.activation(a_hi[:, 0:n * S], a[:, 0:n * S], ACT.Copy).then_inc(a_hi_ok, 1)

            def slice_landed(t, n):
                return w_in[n % 2], 16 * (NJ // 2) * t + 16 * (n // 2 + 1)

            def tile(t, n, back):
                for j in range(NJ):
                    s = NJ * t + j
                    act.wait_ge(up_ok, s + 1)
                    nc.scalar.activation(silu[:, j % 2, 0:n * S], up_ps[:, 0:n * S], ACT.Silu,
                                         bias=w_bias[:, j % RING, 0:1]).then_inc(silu_ok, 1)
                    if back is not None and j == 2:
                        split_a(back[0], back[1])
                    if j == NJ - 1:
                        act.wait_ge(x_in, 16 * G * (t + 2))
                        act.wait_ge(gate_ok, s + 1)
                        split_x(t + 1, n, 0)
                    act.wait_ge(hid_f_ok, s + 1)
                    nc.scalar.activation(hid_hi[:, j % 2, 0:n * S], hid[:, j % 2, 0:n * S],
                                         ACT.Copy).then_inc(hid_hi_ok, 1)
                    if j == NJ - 1:
                        for c in range(1, DC):
                            split_x(t + 1, n, c)
                    landed, count = slice_landed(t, j + AHEAD)
                    act.wait_ge(landed, count)
                    split_slice(j + AHEAD, s)
                for d in range(DC):
                    act.wait_ge(y_f_ok, DC * t + d + 1)
                    nc.scalar.activation(y_hi[:, d, 0:n * S], y[:, d, 0:n * S], ACT.Copy).then_inc(y_hi_ok, 1)

            def finish(t, n, unit0):
                for k in range(AHEAD, LOAD):
                    landed, count = slice_landed(t, NJ + k)
                    act.wait_ge(landed, count)
                split_a(t, n)

            for n in range(AHEAD):
                landed, count = slice_landed(0, n)
                act.wait_ge(landed, count)
                split_slice(n, None)
                if n == 0:
                    act.wait_ge(x_in, 16 * G)
                    for c in range(DC):
                        split_x(0, G, c)
            run(act, whole, last, tile, finish)

        @block.vector
        def _(dve):
            step = [0]

            def link(ins):
                step[0] += 1
                ins.then_inc(routing, 1)
                dve.wait_ge(routing, step[0])

            onehot, ranks, counts, past, moved = (r8[:, k, :] for k in range(1, 6))
            tiles_of, starts, ends = (r16[:, k, :] for k in range(3))
            whole_of, half_of = tiles_of[:, 0:E], tiles_of[:, E:2 * E]

            dve.wait_ge(const_in, 32)
            link(nc.vector.reduce_max(r1[:, 0:1], cond_sb[:, :], AX_X))
            link(nc.vector.scalar_tensor_tensor(out=r8[:, 0, :], in0=cond_sb[:, :], scalar=r1[:, 0:1],
                                                in1=con[:, C_PRIO:C_PRIO + E], op0=ALU.is_equal, op1=ALU.mult))
            link(nc.vector.reduce_max(r1[:, 1:2], r8[:, 0, :], AX_X))
            nc.vector.tensor_scalar(onehot, r8[:, 0, :], r1[:, 1:2], None, ALU.is_equal).then_inc(onehot_ok, 1)
            dve.wait_ge(ranks_ok, 1)
            nc.vector.tensor_copy(ranks, a_ps[:, 0:E])
            link(nc.vector.tensor_copy(counts, o_ps[:, 0:E]))
            more = wide[:, 0:E * (B // G)].rearrange("p (e k) -> p e k", e=E)
            link(nc.vector.tensor_tensor(
                more, counts.unsqueeze(2).to_broadcast([P, E, B // G]),
                con[:, C_FOUR:C_LT].rearrange("p (e k) -> p e k", e=E), ALU.is_gt))
            link(nc.vector.reduce_sum(whole_of, more, AX_X))
            link(nc.vector.scalar_tensor_tensor(out=half_of, in0=whole_of, scalar=float(G), in1=counts,
                                                op0=ALU.mult, op1=ALU.is_lt))
            link(nc.vector.scalar_tensor_tensor(out=past, in0=whole_of, scalar=float(G), in1=ranks,
                                                op0=ALU.mult, op1=ALU.is_le))
            below = wide[:, 512:512 + 4 * E * E].rearrange("p (e k) -> p e k", e=2 * E)
            link(nc.vector.tensor_tensor(
                below, tiles_of.unsqueeze(1).to_broadcast([P, 2 * E, 2 * E]),
                con[:, C_LT:C_TILE].rearrange("p (e k) -> p e k", e=2 * E), ALU.mult))
            link(nc.vector.reduce_sum(starts, below, AX_X))
            link(nc.vector.tensor_tensor(ends, starts, tiles_of, ALU.add))
            link(nc.vector.tensor_tensor(moved, starts[:, E:2 * E], ends[:, 0:E], ALU.subtract))
            link(nc.vector.tensor_tensor(moved, moved, past, ALU.mult))
            link(nc.vector.tensor_tensor(moved, moved, starts[:, 0:E], ALU.add))
            link(nc.vector.scalar_tensor_tensor(out=moved, in0=moved, scalar=float(G), in1=ranks,
                                                op0=ALU.mult, op1=ALU.add))
            link(nc.vector.tensor_tensor(moved, moved, onehot, ALU.mult))
            link(nc.vector.reduce_sum(r1[:, 2:3], moved, AX_X))
            slot_of = wide[:, 0:SLOTS]
            nc.vector.tensor_scalar(slot_of, con[:, C_SLOT:C_SLOT + SLOTS], r1[:, 2:3], None,
                                    ALU.is_equal).then_inc(places_ok, 1)
            passed = wide[0:1, 512:512 + TILES * 2 * E].rearrange("p (t e) -> p t e", e=2 * E)
            link(nc.vector.tensor_tensor(
                passed, con[0:1, C_TILE:C_PRIO].rearrange("p (t e) -> p t e", e=2 * E),
                ends[0:1, :].unsqueeze(1).to_broadcast([1, TILES, 2 * E]), ALU.is_ge))
            number, wrap = wide[0:1, 1280:1280 + TILES], wide[0:1, 1344:1344 + TILES]
            link(nc.vector.reduce_sum(number, passed, AX_X))
            link(nc.vector.tensor_scalar(wrap, number, float(E), float(-E), ALU.is_ge, ALU.mult))
            link(nc.vector.tensor_tensor(number, number, wrap, ALU.add))
            nc.vector.tensor_scalar(table[0:1, T_EXPERT:T_EXPERT + TILES], number, float(E - 1), None, ALU.min)
            nc.vector.tensor_scalar(table[0:1, T_WHOLE:T_WHOLE + 1], ends[0:1, E - 1:E], -1.0, None, ALU.add)
            link(nc.vector.tensor_scalar(r1[0:1, 3:4], ends[0:1, E - 1:E], float(MIN_HALVES), None, ALU.add))
            link(nc.vector.tensor_tensor(r1[0:1, 3:4], r1[0:1, 3:4], ends[0:1, 2 * E - 1:2 * E], ALU.max))
            nc.vector.tensor_scalar(table[0:1, T_LAST:T_LAST + 1], r1[0:1, 3:4], -1.0, None, ALU.add)
            dve.wait_ge(slots_ok, 1)
            link(nc.vector.scalar_tensor_tensor(
                out=wide[0:1, 0:SLOTS], in0=up_ps[0:1, 0:SLOTS], scalar=0.0,
                in1=con[0:1, C_ODD:C_ODD + SLOTS], op0=ALU.is_ge, op1=ALU.mult))
            nc.vector.scalar_tensor_tensor(
                out=table[0:1, T_SLOT:T_SLOT + SLOTS], in0=up_ps[0:1, 0:SLOTS], scalar=float(PAD),
                in1=wide[0:1, 0:SLOTS], op0=ALU.add, op1=ALU.add).then_inc(table_ok, 1)

            dve.wait_ge(l1_in, 16)
            for c in range(DC):
                at = slice(L_BASE + c * D + c * P, L_BASE + c * D + (c + 1) * P)
                ins = nc.vector.tensor_tensor(l1_raw[:, at], l1_raw[:, at], con[:, C_IDENT:C_IDENT + P], ALU.add)
            ins.then_inc(l1_sum, 1)
            dve.wait_ge(l1_hi_ok, 1)
            nc.vector.tensor_tensor(l1_lo[:, :], l1_raw[:, 0:L_MATS], l1_hi[:, :], ALU.subtract).then_inc(l1_ok, 1)
            whole, last = last_tiles(dve)

            def split_slice(s_ahead, n):
                dve.wait_ge(w_hi_ok, s_ahead + 1)
                nc.vector.tensor_copy(w_bias[:, n % RING, :], w_raw[:, n % 2, BIAS:SLICE])
                nc.vector.tensor_tensor(w_lo[:, n % RING, :], w_raw[:, n % 2, 0:BIAS], w_hi[:, n % RING, :],
                                        ALU.subtract).then_inc(w_ok, 1)

            def by_batch(columns, n):
                return columns.rearrange("p (g s) -> p g s", g=n)

            def x_part(t, n, columns):
                return x_raw[:, bass.ds(t % 2, 1), 0:n, columns].rearrange("p o g s -> p (o g) s")

            def split_x(t, n, c):
                dve.wait_ge(x_hi_ok, DC * t + c + 1)
                nc.vector.tensor_tensor(by_batch(x_lo[:, c, 0:n * S], n), x_part(t, n, slice(c * P, (c + 1) * P)),
                                        by_batch(x_hi[:, c, 0:n * S], n), ALU.subtract).then_inc(x_ok, 1)

            def y_sum(t, n, d):
                nc.vector.scalar_tensor_tensor(
                    out=by_batch(y[:, d, 0:n * S], n), in0=by_batch(y_ps[d][:, 0:n * S], n),
                    scalar=w_bias[:, (NJ - 1) % RING, 2 + d:3 + d],
                    in1=x_part(t, n, slice(d * P, (d + 1) * P)),
                    op0=ALU.add, op1=ALU.add).then_inc(y_f_ok, 1)

            def y_low(t, n, d):
                dve.wait_ge(y_hi_ok, DC * t + d + 1)
                nc.vector.tensor_tensor(y_lo[:, d, 0:n * S], y[:, d, 0:n * S], y_hi[:, d, 0:n * S],
                                        ALU.subtract).then_inc(y_ok, 1)

            def weigh_a(t, n):
                dve.wait_ge(a_ps_ok, t + 1)
                nc.vector.scalar_tensor_tensor(
                    out=by_batch(a[:, 0:n * S], n), in0=by_batch(a_ps[:, 0:n * S], n), scalar=SCALING,
                    in1=x_part(t, n, slice(D, XROW)).to_broadcast([P, n, S]),
                    op0=ALU.mult, op1=ALU.mult).then_inc(a_f_ok, 1)

            def split_a(t, n):
                dve.wait_ge(a_hi_ok, t + 1)
                nc.vector.tensor_tensor(a_lo[:, 0:n * S], a[:, 0:n * S], a_hi[:, 0:n * S],
                                        ALU.subtract).then_inc(a_ok, 1)

            def drain_output(unit0, twos, u):
                dve.wait_ge(o_ps_ok, unit0 + u + 1)
                dve.wait_ge(stored[u % 2], 16 * twos + 16 * (u // 2))
                nc.vector.tensor_tensor(o_sb[:, u % 2, :], o_ps[:, :], l1_raw[:, L_BIAS:NL1],
                                        ALU.add).then_inc(o_ok, 1)

            def pairs(t, n):
                return 2 * t if n == G else t + whole + 1

            def tile(t, n, back):
                if back is not None:
                    back_t, back_n, unit0 = back
                for j in range(NJ):
                    s = NJ * t + j
                    if back is not None and j == 2:
                        weigh_a(back_t, back_n)
                        split_a(back_t, back_n)
                    if back is not None and 3 <= j < 3 + back_n:
                        drain_output(unit0, pairs(back_t, back_n), j - 3)
                    dve.wait_ge(gate_ok, s + 1)
                    dve.wait_ge(silu_ok, s + 1)
                    nc.vector.scalar_tensor_tensor(out=hid[:, j % 2, 0:n * S], in0=gate_ps[:, 0:n * S],
                                                   scalar=w_bias[:, j % RING, 1:2], in1=silu[:, j % 2, 0:n * S],
                                                   op0=ALU.add, op1=ALU.mult).then_inc(hid_f_ok, 1)
                    if j == NJ - 1:
                        split_x(t + 1, n, 0)
                    dve.wait_ge(hid_hi_ok, s + 1)
                    nc.vector.tensor_tensor(hid_lo[:, j % 2, 0:n * S], hid[:, j % 2, 0:n * S],
                                            hid_hi[:, j % 2, 0:n * S], ALU.subtract).then_inc(hid_ok, 1)
                    if j == NJ - 1:
                        for c in range(1, DC):
                            split_x(t + 1, n, c)
                    if (j + AHEAD) % RING == (NJ - 1) % RING:
                        dve.wait_ge(y_f_ok, DC * t)
                    split_slice(s + AHEAD, j + AHEAD)
                dve.wait_ge(down_ok, NJ * (t + 1))
                dve.wait_ge(y_ok, DC * t)
                for d in range(DC):
                    y_sum(t, n, d)
                for d in range(DC):
                    y_low(t, n, d)

            def finish(t, n, unit0):
                weigh_a(t, n)
                split_a(t, n)
                for u in range(n):
                    drain_output(unit0, pairs(t, n), u)

            for n in range(AHEAD):
                split_slice(n, n)
                if n == 0:
                    for c in range(DC):
                        split_x(0, G, c)
            run(dve, whole, last, tile, finish)


def lay_out(x, cond_8, W_up, b_up, W_gate, b_gate, W_down, b_down, W_base, b_base, As, Bs):
    xt = np.zeros((B + 2, P, XROW), np.float32)
    xt[:B, :, :D] = x.reshape(B, S, DC, P).transpose(0, 3, 2, 1).reshape(B, P, D)
    xt[:B, :, D] = np.repeat(cond_8, R, axis=1)
    we = np.empty((E, NJ, P, SLICE), np.float32)
    for at, w in ((UP, W_up), (GATE, W_gate)):
        we[..., at:at + D] = w.reshape(E, NJ, P, DC, P).transpose(0, 1, 4, 3, 2).reshape(E, NJ, P, D)
    we[..., DOWN:BIAS] = W_down.reshape(E, D, NJ, P).transpose(0, 2, 3, 1)
    we[..., BIAS] = b_up.reshape(E, NJ, P)
    we[..., BIAS + 1] = b_gate.reshape(E, NJ, P)
    we[..., BIAS + 2:] = b_down.reshape(E, 1, DC, P).transpose(0, 1, 3, 2)
    l1 = np.empty((P, NL1), np.float32)
    l1[:, L_BASE:L_A] = W_base.reshape(D, DC, P).transpose(2, 1, 0).reshape(P, DC * D)
    l1[:, L_A:L_B] = As.reshape(E * R, DC, P).transpose(2, 1, 0).reshape(P, DC * P)
    l1[:, L_B:L_BIAS] = Bs.transpose(0, 2, 1).reshape(E * R, D)
    l1[:, L_BIAS:] = b_base[None, :]
    return {"xt": xt, "we": we, "cond": np.ascontiguousarray(cond_8), "l1": l1, "consts": constants()}


def kernel(x, cond_8, L0_cond_W_up, L0_cond_b_up, L0_cond_W_gate, L0_cond_b_gate, L0_cond_W_down,
           L0_cond_b_down, L1_cond_W_base, L1_cond_b_base, L1_cond_As, L1_cond_Bs):
    import concourse.bacc as bacc
    from concourse.bass_utils import run_bass_kernel_spmd

    arrays = lay_out(*(np.asarray(v) for v in (
        x, cond_8, L0_cond_W_up, L0_cond_b_up, L0_cond_W_gate, L0_cond_b_gate, L0_cond_W_down,
        L0_cond_b_down, L1_cond_W_base, L1_cond_b_base, L1_cond_As, L1_cond_Bs)))
    nc = bacc.Bacc("TRN2", target_bir_lowering=False, num_devices=1)
    aps = [nc.dram_tensor(k, v.shape, F32, kind="ExternalInput").ap() for k, v in arrays.items()]
    out = nc.dram_tensor("out", (B + 2, S, D), F32, kind="ExternalOutput").ap()
    build(nc, *aps, out)
    got = run_bass_kernel_spmd(nc, [arrays], core_ids=[0])
    return got.results[0]["out"][:B]
```

```python
from contextlib import ExitStack

import numpy as np

import concourse.bass as bass
from concourse import mybir

ALU = mybir.AluOpType
ACT = mybir.ActivationFunctionType
AX_X = mybir.AxisListType.X
F32 = mybir.dt.float32
F32R = mybir.dt.float32r
I32 = mybir.dt.int32

P = 128
B, S, D = 128, 128, 512
E, H = 8, 1024
R = 16
DC = D // P
NJ = H // P
G = 4
REST = range(G - 1, 1, -1)
KINDS = 1 + len(REST)
LEAST = min(REST)
N = G * S
SCALING = 32.0 / R

UP, GATE, DOWN, BIAS = 0, D, 2 * D, 3 * D
NBIAS = 2 + DC
SLICE = 3 * D + NBIAS
XROW = D + 1

MIN_WHOLE = (B - (G + 1) * E) // G
MAXT = (B + (G - 1) * E) // G
TILES = MAXT + 2
SLOTS = TILES * G
RING = 4
AHEAD = RING - 1
LOAD = AHEAD + 2
PAD = B

T_LAST, T_COUNT, T_EXPERT, T_SLOT = 0, 4, 8, 64
TABLE = T_SLOT + SLOTS

A_TRI, A_ONES, A_BATCH, A_TILE = 0, P, 2 * P, 2 * P + 1
NCON_A = A_TILE + 1
B_FOUR = 0
B_SLOT = B_FOUR + E * (B // G)
B_IDENT = B_SLOT + SLOTS
NCON_B = B_IDENT + P

L_BASE, L_A, L_B, L_BIAS = 0, DC * D, DC * D + DC * P, DC * D + DC * P + D
L_MATS = L_BIAS
L_PARTS = 2
L_PART = L_MATS // L_PARTS
NL1 = L_BIAS + D


def constants():
    a = np.ones((P, NCON_A), np.float32)
    a[:, A_TRI:A_TRI + P] = np.arange(P)[:, None] < np.arange(P)[None, :]
    a[:, A_BATCH] = np.arange(B) - PAD
    a[:, A_TILE] = np.arange(P)
    b = np.empty((P, NCON_B), np.float32)
    b[:, B_FOUR:B_SLOT] = np.tile(G * np.arange(B // G) + G - 1, E)
    b[:, B_SLOT:B_IDENT] = np.arange(SLOTS)
    b[:, B_IDENT:] = np.eye(P)
    return {"con_a": a, "con_b": b}


def build(nc, xt, we, cond, l1, consts_a, consts_b, out):
    with ExitStack() as ctx:
        def sb(name, shape, dt=F32):
            return ctx.enter_context(nc.sbuf_tensor(name, shape, dt))

        def bank(name):
            return ctx.enter_context(nc.psum_tensor(name, [P, N], F32))

        def sem(name):
            return ctx.enter_context(nc.semaphore(name))

        w_hi = sb("w_hi", [P, RING, 3 * D], F32R)
        w_lo = sb("w_lo", [P, RING, 3 * D], F32R)
        w_raw = sb("w_raw", [P, 2, SLICE])
        w_bias = sb("w_bias", [P, RING, NBIAS])
        l1_raw = sb("l1_raw", [P, NL1])
        l1_hi = sb("l1_hi", [P, L_MATS], F32R)
        l1_lo = sb("l1_lo", [P, L_MATS], F32R)
        x_raw = sb("x_raw", [P, 2, G, XROW])
        x_hi = sb("x_hi", [P, DC, N], F32R)
        x_lo = sb("x_lo", [P, DC, N], F32R)
        silu = sb("silu", [P, 2, N])
        hid = sb("hid", [P, 2, N])
        hid_hi = sb("hid_hi", [P, 2, N], F32R)
        hid_lo = sb("hid_lo", [P, 2, N], F32R)
        y = sb("y", [P, DC, N])
        y_hi = sb("y_hi", [P, DC, N], F32R)
        y_lo = sb("y_lo", [P, DC, N], F32R)
        a = sb("a", [P, N])
        a_hi = sb("a_hi", [P, N], F32R)
        a_lo = sb("a_lo", [P, N], F32R)
        o_sb = sb("o_sb", [P, G, D])
        con_a, con_b = sb("con_a", [P, NCON_A]), sb("con_b", [P, NCON_B])
        cond_sb = sb("cond_sb", [P, 2 * E])
        r8 = sb("r8", [P, 8, E])
        r_kinds = sb("r_kinds", [P, 3, KINDS, E])
        r1 = sb("r1", [P, 4])
        table = sb("table", [1, TABLE], I32)
        wide = x_raw[:, :, :, :].rearrange("p a g n -> p (a g n)")

        up_ps, gate_ps, a_ps, o_ps = bank("up_ps"), bank("gate_ps"), bank("a_ps"), bank("o_ps")
        y_ps = [bank(f"y_ps{d}") for d in range(DC)]

        cond_in, con_a_in, con_b_in, l1_in = sem("cond_in"), sem("con_a_in"), sem("con_b_in"), sem("l1_in")
        routing, onehot_ok, ranks_ok, places_ok = sem("routing"), sem("onehot_ok"), sem("ranks_ok"), sem("places_ok")
        numbers_ok, slots_ok, experts_ok, table_ok = sem("numbers_ok"), sem("slots_ok"), sem("experts_ok"), sem("table_ok")
        l1_sum, l1_hi_ok, l1_ok = sem("l1_sum"), sem("l1_hi_ok"), sem("l1_ok")
        w_in = [sem("w_in0"), sem("w_in1")]
        x_in = sem("x_in")
        w_hi_ok, w_ok = sem("w_hi_ok"), sem("w_ok")
        x_hi_ok, x_ok = sem("x_hi_ok"), sem("x_ok")
        up_ok, gate_ok, down_ok = sem("up_ok"), sem("gate_ok"), sem("down_ok")
        silu_ok, hid_f_ok, hid_hi_ok, hid_ok = sem("silu_ok"), sem("hid_f_ok"), sem("hid_hi_ok"), sem("hid_ok")
        y_f_ok, y_hi_ok, y_ok = sem("y_f_ok"), sem("y_hi_ok"), sem("y_ok")
        a_ps_ok, a_f_ok, a_hi_ok, a_ok = sem("a_ps_ok"), sem("a_f_ok"), sem("a_hi_ok"), sem("a_ok")
        o_ps_ok = [sem(f"o_ps_ok{u}") for u in range(G)]
        o_ok = [sem(f"o_ok{u}") for u in range(G)]
        stored = [sem(f"stored{u}") for u in range(G)]

        block = ctx.enter_context(nc.Block())

        def routed(eng):
            eng.wait_ge(table_ok, 1)
            last = {n: eng.value_load(table[0:1, T_LAST + G - n:T_LAST + G - n + 1], min_val=MIN_WHOLE - 1,
                                      max_val=MAXT - 1) for n in (G, *REST)}
            count = {n: eng.value_load(table[0:1, T_COUNT + G - n:T_COUNT + G - n + 1], min_val=0,
                                       max_val=E) for n in REST}
            return last, count

        def slice_landed(t, n):
            return w_in[n % 2], 16 * (NJ // 2) * t + 16 * (n // 2 + 1)

        def run(eng, plan, tile, second_layer):
            last, count = plan
            tile(0, G, None)
            with eng.Fori(1, last[G] + 1) as t:
                tile(t, G, t - 1)
            second_layer(last[G], G)
            for n in REST:
                with eng.If(count[n]):
                    tile(last[n + 1] + 1, n, None)
                    with eng.If(count[n] - 1):
                        with eng.Fori(last[n + 1] + 2, last[n] + 1) as t:
                            tile(t, n, t - 1)
                    second_layer(last[n], n)

        @block.sync
        def _(sp):
            sp.dma_start(cond_sb[:, :], cond).then_inc(cond_in, 16)
            sp.dma_start(con_a[:, :], consts_a).then_inc(con_a_in, 16)
            sp.dma_start(l1_raw[:, :], l1).then_inc(l1_in, 16)

            def expert(t):
                return sp.value_load(table[0:1, bass.ds(T_EXPERT + t, 1)], min_val=0, max_val=E - 1)

            def batches(t, n, most):
                return [sp.value_load(table[0:1, bass.ds(T_SLOT + G * t + i, 1)], min_val=0, max_val=most)
                        for i in range(n)]

            def load_slice(e, j, n):
                sp.dma_start(w_raw[:, n % 2, :], we[e, j]).then_inc(w_in[n % 2], 16)

            def load_x(t, b):
                for i, batch in enumerate(b):
                    sp.dma_start(x_raw[:, bass.ds(t % 2, 1), i, :], xt[batch]).then_inc(
                        x_in, 16 if i + 1 < len(b) else 16 * (G - i))

            def store(t, u, batch):
                sp.wait_ge(o_ok[u], t + 1)
                sp.wait_ge(table_ok, 1)
                sp.dma_start(out[batch], o_sb[:, u, :]).then_inc(stored[u], 16)

            def tile(t, n, back):
                here, after = expert(t), expert(t + 1)
                ahead = batches(t + 1, n, PAD)
                if back is not None:
                    back_b = batches(back, n, PAD)
                for j in range(NJ):
                    sp.wait_ge(w_ok, NJ * t + j + AHEAD + 1)
                    sp.wait_ge(table_ok, 1)
                    k = j + LOAD
                    load_slice(here if k < NJ else after, k % NJ, k)
                    if j == 2:
                        sp.wait_ge(a_f_ok, t)
                        sp.wait_ge(table_ok, 1)
                        load_x(t + 1, ahead)
                    if back is not None and 3 <= j < 2 + n:
                        store(back, j - 3, back_b[j - 3])
                if back is not None:
                    store(back, n - 1, back_b[n - 1])

            def second_layer(t, n):
                b = batches(t, n, PAD)
                for u in range(n):
                    store(t, u, b[u])

            sp.wait_ge(experts_ok, 1)
            e0 = expert(0)
            load_slice(e0, 0, 0)
            sp.wait_ge(table_ok, 1)
            load_x(0, batches(0, G, PAD))
            load_slice(e0, 1, 1)
            plan = routed(sp)
            for n in range(2, LOAD):
                sp.wait_ge(w_ok, n - 1)
                load_slice(e0, n, n)
            run(sp, plan, tile, second_layer)

        @block.gpsimd
        def _(pool):
            last, _ = routed(pool)
            for k in range(AHEAD, LOAD):
                landed, count = slice_landed(last[LEAST] + 1, k)
                pool.wait_ge(landed, count)
            for u in range(G):
                pool.wait_ge(stored[u], 16 * (last[max(u + 1, LEAST)] + 1))

        @block.tensor
        def _(pe):
            pe.wait_ge(con_a_in, 16)
            pe.wait_ge(onehot_ok, 1)
            nc.tensor.matmul(a_ps[:, 0:E], con_a[:, A_TRI:A_TRI + P], r8[:, 1, :], start=True, stop=True)
            nc.tensor.matmul(o_ps[:, 0:E], con_a[:, A_ONES:A_ONES + P], r8[:, 1, :], start=True,
                             stop=True).then_inc(ranks_ok, 1)
            pe.wait_ge(con_b_in, 16)
            pe.wait_ge(numbers_ok, 1)
            nc.tensor.matmul(gate_ps[0:1, 0:P], r1[:, 3:4], con_b[:, B_IDENT:NCON_B], start=True,
                             stop=True).then_inc(slots_ok, 1)
            pe.wait_ge(places_ok, 1)
            nc.tensor.matmul(up_ps[0:1, 0:SLOTS], con_a[:, A_BATCH:A_BATCH + 1], wide[:, 0:SLOTS], start=True,
                             stop=True).then_inc(slots_ok, 1)
            plan = routed(pe)

            def product(ps, left_hi, left_lo, right_hi, right_lo, start, stop):
                nc.tensor.matmul(ps, left_hi, right_hi, start=start, stop=False)
                nc.tensor.matmul(ps, left_hi, right_lo, start=False, stop=False)
                return nc.tensor.matmul(ps, left_lo, right_hi, start=False, stop=stop)

            def up_or_gate(ps, t, n, j, at, done):
                k = j % RING
                for c in range(DC):
                    if at == UP and j == 0:
                        pe.wait_ge(x_ok, DC * t + c + 1)
                    w = slice(at + c * P, at + (c + 1) * P)
                    ins = product(ps[:, 0:n * S], w_hi[:, k, w], w_lo[:, k, w], x_hi[:, c, 0:n * S], x_lo[:, c, 0:n * S],
                                   c == 0, c == DC - 1)
                ins.then_inc(done, 1)

            def sums_free(n, t):
                for m in range(G, n, -1):
                    pe.wait_ge(o_ok[m - 1], plan[0][m] + 1)
                pe.wait_ge(o_ok[n - 1], t)

            def down(t, n, j, back):
                pe.wait_ge(hid_ok, NJ * t + j + 1)
                if j == 0:
                    pe.wait_ge(y_f_ok, DC * t)
                    if back is None and n < G:
                        sums_free(n, t)
                k = j % RING
                for d in range(DC):
                    w = slice(DOWN + d * P, DOWN + (d + 1) * P)
                    ins = product(y_ps[d][:, 0:n * S], w_hi[:, k, w], w_lo[:, k, w], hid_hi[:, j % 2, 0:n * S],
                                   hid_lo[:, j % 2, 0:n * S], j == 0, j == NJ - 1)
                ins.then_inc(down_ok, 1)

            def lora_a(t, n):
                pe.wait_ge(l1_ok, L_PARTS)
                pe.wait_ge(a_f_ok, t)
                for c in range(DC):
                    pe.wait_ge(y_ok, DC * t + c + 1)
                    w = slice(L_A + c * P, L_A + (c + 1) * P)
                    ins = product(a_ps[:, 0:n * S], l1_hi[:, w], l1_lo[:, w], y_hi[:, c, 0:n * S], y_lo[:, c, 0:n * S],
                                   c == 0, c == DC - 1)
                ins.then_inc(a_ps_ok, 1)

            def outputs(t, n, u, alone):
                ps = y_ps[u] if alone else o_ps
                if not alone and u:
                    pe.wait_ge(o_ok[u - 1], t + 1)
                elif not alone:
                    pe.wait_ge(o_ok[n - 1], t)
                rows = slice(u * S, (u + 1) * S)
                for c in range(DC):
                    w = slice(L_BASE + c * D, L_BASE + (c + 1) * D)
                    product(ps[:, :], y_hi[:, c, rows], y_lo[:, c, rows], l1_hi[:, w], l1_lo[:, w],
                            c == 0, False)
                pe.wait_ge(a_ok, t + 1)
                w = slice(L_B, L_B + D)
                product(ps[:, :], a_hi[:, rows], a_lo[:, rows], l1_hi[:, w], l1_lo[:, w],
                        False, True).then_inc(o_ps_ok[u], 1)

            def tile(t, n, back):
                for j in range(NJ):
                    pe.wait_ge(w_ok, NJ * t + j + 1)
                    pe.wait_ge(silu_ok, NJ * t + j)
                    up_or_gate(up_ps, t, n, j, UP, up_ok)
                    pe.wait_ge(hid_f_ok, NJ * t + j)
                    up_or_gate(gate_ps, t, n, j, GATE, gate_ok)
                    if j >= 1:
                        down(t, n, j - 1, back)
                    if back is not None and j == 1:
                        lora_a(back, n)
                    if back is not None and 2 <= j < 1 + n:
                        outputs(back, n, j - 2, False)
                if back is not None:
                    outputs(back, n, n - 1, False)
                down(t, n, NJ - 1, back)

            def second_layer(t, n):
                lora_a(t, n)
                pe.wait_ge(y_f_ok, DC * (t + 1))
                for u in range(n):
                    outputs(t, n, u, True)

            run(pe, plan, tile, second_layer)

        @block.scalar
        def _(act):
            act.dma_start(con_b[:, :], consts_b).then_inc(con_b_in, 16)
            plan = routed(act)

            def split_slice(n, freed):
                if freed is not None:
                    act.wait_ge(down_ok, freed)
                nc.scalar.activation(w_hi[:, n % RING, :], w_raw[:, n % 2, 0:BIAS], ACT.Copy).then_inc(w_hi_ok, 1)

            def split_x(t, n, c):
                nc.scalar.activation(x_hi[:, c, 0:n * S].rearrange("p (g s) -> p g s", g=n),
                                     x_raw[:, bass.ds(t % 2, 1), 0:n, c * P:(c + 1) * P].rearrange(
                                         "p o g s -> p (o g) s"),
                                     ACT.Copy).then_inc(x_hi_ok, 1)

            def split_a(t, n):
                act.wait_ge(a_f_ok, t + 1)
                nc.scalar.activation(a_hi[:, 0:n * S], a[:, 0:n * S], ACT.Copy).then_inc(a_hi_ok, 1)

            def split_l1(part):
                act.wait_ge(l1_sum, 1)
                at = slice(part * L_PART, (part + 1) * L_PART)
                nc.scalar.activation(l1_hi[:, at], l1_raw[:, at], ACT.Copy).then_inc(l1_hi_ok, 1)

            def split_y(t, n, chunks):
                for d in chunks:
                    act.wait_ge(y_f_ok, DC * t + d + 1)
                    nc.scalar.activation(y_hi[:, d, 0:n * S], y[:, d, 0:n * S], ACT.Copy).then_inc(y_hi_ok, 1)

            def split_ahead(t, j):
                landed, count = slice_landed(t, j + AHEAD)
                act.wait_ge(landed, count)
                split_slice(j + AHEAD, NJ * t + j)

            def tile(t, n, back):
                for j in range(NJ):
                    s = NJ * t + j
                    act.wait_ge(up_ok, s + 1)
                    nc.scalar.activation(silu[:, j % 2, 0:n * S], up_ps[:, 0:n * S], ACT.Silu,
                                         bias=w_bias[:, j % RING, 0:1]).then_inc(silu_ok, 1)
                    if back is not None and j == 0:
                        split_y(back, n, range(DC // 2, DC))
                    if back is not None and j == 2:
                        split_a(back, n)
                    if j == NJ - 1:
                        act.wait_ge(x_in, 16 * G * (t + 2))
                        act.wait_ge(gate_ok, s + 1)
                        split_x(t + 1, n, 0)
                    act.wait_ge(hid_f_ok, s + 1)
                    nc.scalar.activation(hid_hi[:, j % 2, 0:n * S], hid[:, j % 2, 0:n * S],
                                         ACT.Copy).then_inc(hid_hi_ok, 1)
                    if j == NJ - 1:
                        for c in range(1, DC):
                            split_x(t + 1, n, c)
                    split_ahead(t, j)
                    if back is None and n == G and 2 <= j < 2 + L_PARTS:
                        split_l1(j - 2)
                split_y(t, n, range(DC // 2))

            def second_layer(t, n):
                split_y(t, n, range(DC // 2, DC))
                split_a(t, n)

            for n in range(AHEAD):
                landed, count = slice_landed(0, n)
                act.wait_ge(landed, count)
                split_slice(n, None)
                if n == 0:
                    act.wait_ge(x_in, 16 * G)
                    for c in range(DC):
                        split_x(0, G, c)
            run(act, plan, tile, second_layer)

        @block.vector
        def _(dve):
            step = [0]

            def link(ins):
                step[0] += 1
                ins.then_inc(routing, 1)
                dve.wait_ge(routing, step[0])

            onehot, ranks, counts, left, moved, behind, pair = (r8[:, k, :] for k in range(1, 8))
            tiles_of, starts, ends = (r_kinds[:, k, :, :] for k in range(3))
            flat = [r_kinds[:, k, :, :].rearrange("p k e -> p (k e)") for k in range(3)]

            dve.wait_ge(cond_in, 16)
            link(nc.vector.reduce_max(r1[:, 0:1], cond_sb[:, 0:E], AX_X))
            link(nc.vector.scalar_tensor_tensor(out=r8[:, 0, :], in0=cond_sb[:, 0:E], scalar=r1[:, 0:1],
                                                in1=cond_sb[:, E:2 * E], op0=ALU.is_equal, op1=ALU.mult))
            link(nc.vector.reduce_max(r1[:, 1:2], r8[:, 0, :], AX_X))
            nc.vector.tensor_scalar(onehot, r8[:, 0, :], r1[:, 1:2], None, ALU.is_equal).then_inc(onehot_ok, 1)
            dve.wait_ge(ranks_ok, 1)
            nc.vector.tensor_copy(ranks, a_ps[:, 0:E])
            link(nc.vector.tensor_copy(counts, o_ps[:, 0:E]))
            dve.wait_ge(con_b_in, 16)
            more = wide[:, 0:E * (B // G)].rearrange("p (e k) -> p e k", e=E)
            link(nc.vector.tensor_tensor(
                more, counts.unsqueeze(2).to_broadcast([P, E, B // G]),
                con_b[:, B_FOUR:B_SLOT].rearrange("p (e k) -> p e k", e=E), ALU.is_gt))
            link(nc.vector.reduce_sum(tiles_of[:, 0, :], more, AX_X))
            link(nc.vector.scalar_tensor_tensor(out=left, in0=tiles_of[:, 0, :], scalar=float(-G), in1=counts,
                                                op0=ALU.mult, op1=ALU.add))
            link(nc.vector.tensor_scalar(pair, counts, float(G), None, ALU.is_gt))
            link(nc.vector.scalar_tensor_tensor(out=pair, in0=left, scalar=1.0, in1=pair,
                                                op0=ALU.is_equal, op1=ALU.mult))
            nc.vector.tensor_tensor(tiles_of[:, 0, :], tiles_of[:, 0, :], pair, ALU.subtract)
            link(nc.vector.scalar_tensor_tensor(out=left, in0=pair, scalar=float(G), in1=left,
                                                op0=ALU.mult, op1=ALU.add))
            nc.vector.tensor_scalar(tiles_of[:, 1, :], left, 3.0, None, ALU.is_ge)
            link(nc.vector.scalar_tensor_tensor(out=tiles_of[:, 2, :], in0=left, scalar=3.0, in1=left,
                                                op0=ALU.not_equal, op1=ALU.mult))
            link(nc.vector.tensor_scalar(tiles_of[:, 2, :], tiles_of[:, 2, :], 0.0, None, ALU.is_gt))
            dve.wait_ge(con_a_in, 16)
            link(nc.vector.tensor_tensor_scan(flat[2], con_a[:, A_ONES:A_ONES + KINDS * E], flat[0], 0.0,
                                              ALU.mult, ALU.add))
            link(nc.vector.tensor_tensor(starts, ends, tiles_of, ALU.subtract))
            link(nc.vector.tensor_scalar(wide[:, 0:KINDS * E], flat[2], con_a[:, A_TILE:A_TILE + 1], None,
                                         ALU.is_le))
            nc.vector.reduce_sum(r1[:, 3:4], wide[:, 0:KINDS * E], AX_X).then_inc(numbers_ok, 1)
            link(nc.vector.scalar_tensor_tensor(out=behind, in0=tiles_of[:, 0, :], scalar=float(-G), in1=ranks,
                                                op0=ALU.mult, op1=ALU.add))
            link(nc.vector.tensor_tensor(moved, starts[:, 1, :], ends[:, 0, :], ALU.subtract))
            link(nc.vector.scalar_tensor_tensor(out=moved, in0=behind, scalar=0.0, in1=moved,
                                                op0=ALU.is_ge, op1=ALU.mult))
            link(nc.vector.tensor_tensor(moved, moved, starts[:, 0, :], ALU.add))
            link(nc.vector.scalar_tensor_tensor(out=moved, in0=moved, scalar=float(G), in1=ranks,
                                                op0=ALU.mult, op1=ALU.add))
            experts = table[0:1, T_EXPERT:T_EXPERT + TILES]
            dve.wait_ge(slots_ok, 1)
            link(nc.vector.tensor_copy(experts, gate_ps[0:1, 0:TILES]))
            nc.vector.tensor_scalar(experts, experts, E - 1, None, ALU.bitwise_and).then_inc(experts_ok, 1)
            threes, on = left, pair
            link(nc.vector.tensor_scalar(threes, tiles_of[:, 1, :], 3.0, None, ALU.mult))
            link(nc.vector.tensor_tensor(on, starts[:, 2, :], starts[:, 1, :], ALU.subtract))
            link(nc.vector.scalar_tensor_tensor(out=on, in0=on, scalar=float(G), in1=threes,
                                                op0=ALU.mult, op1=ALU.subtract))
            link(nc.vector.tensor_tensor(behind, behind, threes, ALU.is_ge))
            link(nc.vector.tensor_tensor(on, on, behind, ALU.mult))
            link(nc.vector.tensor_tensor(moved, moved, on, ALU.add))
            link(nc.vector.tensor_tensor(moved, moved, onehot, ALU.mult))
            link(nc.vector.reduce_sum(r1[:, 2:3], moved, AX_X))
            nc.vector.tensor_scalar(wide[:, 0:SLOTS], con_b[:, B_SLOT:B_IDENT], r1[:, 2:3], None,
                                    ALU.is_equal).then_inc(places_ok, 1)
            nc.vector.tensor_scalar(table[0:1, T_LAST:T_LAST + KINDS], ends[0:1, :, E - 1], -1.0, None, ALU.add)
            nc.vector.tensor_tensor(table[0:1, T_COUNT:T_COUNT + KINDS], ends[0:1, :, E - 1],
                                    starts[0:1, :, 0], ALU.subtract)
            dve.wait_ge(slots_ok, 2)
            nc.vector.tensor_scalar(table[0:1, T_SLOT:T_SLOT + SLOTS], up_ps[0:1, 0:SLOTS], float(PAD), None,
                                    ALU.add).then_inc(table_ok, 1)

            dve.wait_ge(l1_in, 16)
            for c in range(DC):
                at = slice(L_BASE + c * D + c * P, L_BASE + c * D + (c + 1) * P)
                ins = nc.vector.tensor_tensor(l1_raw[:, at], l1_raw[:, at], con_b[:, B_IDENT:NCON_B], ALU.add)
            ins.then_inc(l1_sum, 1)
            plan = routed(dve)

            def split_slice(s_ahead, n):
                dve.wait_ge(w_hi_ok, s_ahead + 1)
                nc.vector.tensor_copy(w_bias[:, n % RING, :], w_raw[:, n % 2, BIAS:SLICE])
                nc.vector.tensor_tensor(w_lo[:, n % RING, :], w_raw[:, n % 2, 0:BIAS], w_hi[:, n % RING, :],
                                        ALU.subtract).then_inc(w_ok, 1)

            def by_batch(columns, n):
                return columns.rearrange("p (g s) -> p g s", g=n)

            def x_part(t, n, columns):
                return x_raw[:, bass.ds(t % 2, 1), 0:n, columns].rearrange("p o g s -> p (o g) s")

            def split_x(t, n, c):
                dve.wait_ge(x_hi_ok, DC * t + c + 1)
                nc.vector.tensor_tensor(by_batch(x_lo[:, c, 0:n * S], n), x_part(t, n, slice(c * P, (c + 1) * P)),
                                        by_batch(x_hi[:, c, 0:n * S], n), ALU.subtract).then_inc(x_ok, 1)

            def y_sum(t, n, d):
                nc.vector.scalar_tensor_tensor(
                    out=by_batch(y[:, d, 0:n * S], n), in0=by_batch(y_ps[d][:, 0:n * S], n),
                    scalar=w_bias[:, (NJ - 1) % RING, 2 + d:3 + d],
                    in1=x_part(t, n, slice(d * P, (d + 1) * P)),
                    op0=ALU.add, op1=ALU.add).then_inc(y_f_ok, 1)

            def y_low(t, n, d):
                dve.wait_ge(y_hi_ok, DC * t + d + 1)
                nc.vector.tensor_tensor(y_lo[:, d, 0:n * S], y[:, d, 0:n * S], y_hi[:, d, 0:n * S],
                                        ALU.subtract).then_inc(y_ok, 1)

            def split_l1(part):
                dve.wait_ge(l1_hi_ok, part + 1)
                at = slice(part * L_PART, (part + 1) * L_PART)
                nc.vector.tensor_tensor(l1_lo[:, at], l1_raw[:, at], l1_hi[:, at], ALU.subtract).then_inc(l1_ok, 1)

            def finish_y(t, n):
                for d in range(DC // 2, DC):
                    y_low(t, n, d)

            def weigh_a(t, n):
                dve.wait_ge(a_ps_ok, t + 1)
                nc.vector.scalar_tensor_tensor(
                    out=by_batch(a[:, 0:n * S], n), in0=by_batch(a_ps[:, 0:n * S], n), scalar=SCALING,
                    in1=x_part(t, n, slice(D, XROW)).to_broadcast([P, n, S]),
                    op0=ALU.mult, op1=ALU.mult).then_inc(a_f_ok, 1)

            def split_a(t, n):
                dve.wait_ge(a_hi_ok, t + 1)
                nc.vector.tensor_tensor(a_lo[:, 0:n * S], a[:, 0:n * S], a_hi[:, 0:n * S],
                                        ALU.subtract).then_inc(a_ok, 1)

            def drain_output(t, u, ps):
                dve.wait_ge(o_ps_ok[u], t + 1)
                dve.wait_ge(stored[u], 16 * t)
                nc.vector.tensor_tensor(o_sb[:, u, :], ps[:, :], l1_raw[:, L_BIAS:NL1],
                                        ALU.add).then_inc(o_ok[u], 1)

            def split_ahead(t, j):
                if (j + AHEAD) % RING == (NJ - 1) % RING:
                    dve.wait_ge(y_f_ok, DC * t)
                split_slice(NJ * t + j + AHEAD, j + AHEAD)

            def tile(t, n, back):
                if back is not None:
                    finish_y(back, n)
                for j in range(NJ):
                    s = NJ * t + j
                    if back is not None and j == 2:
                        weigh_a(back, n)
                        split_a(back, n)
                    if back is not None and 3 <= j < 2 + n:
                        drain_output(back, j - 3, o_ps)
                    dve.wait_ge(gate_ok, s + 1)
                    dve.wait_ge(silu_ok, s + 1)
                    nc.vector.scalar_tensor_tensor(out=hid[:, j % 2, 0:n * S], in0=gate_ps[:, 0:n * S],
                                                   scalar=w_bias[:, j % RING, 1:2], in1=silu[:, j % 2, 0:n * S],
                                                   op0=ALU.add, op1=ALU.mult).then_inc(hid_f_ok, 1)
                    if j == NJ - 1:
                        split_x(t + 1, n, 0)
                    dve.wait_ge(hid_hi_ok, s + 1)
                    nc.vector.tensor_tensor(hid_lo[:, j % 2, 0:n * S], hid[:, j % 2, 0:n * S],
                                            hid_hi[:, j % 2, 0:n * S], ALU.subtract).then_inc(hid_ok, 1)
                    if j == NJ - 1:
                        for c in range(1, DC):
                            split_x(t + 1, n, c)
                    split_ahead(t, j)
                    if back is None and n == G and 2 <= j < 2 + L_PARTS:
                        split_l1(j - 2)
                if back is not None:
                    drain_output(back, n - 1, o_ps)
                dve.wait_ge(down_ok, NJ * (t + 1))
                dve.wait_ge(y_ok, DC * t)
                y_sum(t, n, 0)
                y_sum(t, n, 1)
                y_low(t, n, 0)
                for d in range(2, DC):
                    y_sum(t, n, d)
                y_low(t, n, 1)

            def second_layer(t, n):
                finish_y(t, n)
                weigh_a(t, n)
                split_a(t, n)
                for u in range(n):
                    drain_output(t, u, y_ps[u])

            for n in range(AHEAD):
                split_slice(n, n)
                if n == 0:
                    for c in range(DC):
                        split_x(0, G, c)
            run(dve, plan, tile, second_layer)


def lay_out(x, cond_8, W_up, b_up, W_gate, b_gate, W_down, b_down, W_base, b_base, As, Bs):
    xt = np.zeros((B + 1, P, XROW), np.float32)
    xt[:B, :, :D] = x.reshape(B, S, DC, P).transpose(0, 3, 2, 1).reshape(B, P, D)
    xt[:B, :, D] = np.repeat(cond_8, R, axis=1)
    we = np.empty((E, NJ, P, SLICE), np.float32)
    for at, w in ((UP, W_up), (GATE, W_gate)):
        we[..., at:at + D] = w.reshape(E, NJ, P, DC, P).transpose(0, 1, 4, 3, 2).reshape(E, NJ, P, D)
    we[..., DOWN:BIAS] = W_down.reshape(E, D, NJ, P).transpose(0, 2, 3, 1)
    we[..., BIAS] = b_up.reshape(E, NJ, P)
    we[..., BIAS + 1] = b_gate.reshape(E, NJ, P)
    we[..., BIAS + 2:] = b_down.reshape(E, 1, DC, P).transpose(0, 1, 3, 2)
    l1 = np.empty((P, NL1), np.float32)
    l1[:, L_BASE:L_A] = W_base.reshape(D, DC, P).transpose(2, 1, 0).reshape(P, DC * D)
    l1[:, L_A:L_B] = As.reshape(E * R, DC, P).transpose(2, 1, 0).reshape(P, DC * P)
    l1[:, L_B:L_BIAS] = Bs.transpose(0, 2, 1).reshape(E * R, D)
    l1[:, L_BIAS:] = b_base[None, :]
    cond = np.concatenate([cond_8, np.broadcast_to(E - np.arange(E, dtype=np.float32), (B, E))], axis=1)
    return {"xt": xt, "we": we, "cond": cond, "l1": l1} | constants()


def kernel(x, cond_8, L0_cond_W_up, L0_cond_b_up, L0_cond_W_gate, L0_cond_b_gate, L0_cond_W_down,
           L0_cond_b_down, L1_cond_W_base, L1_cond_b_base, L1_cond_As, L1_cond_Bs):
    import concourse.bacc as bacc
    from concourse.bass_utils import run_bass_kernel_spmd

    arrays = lay_out(*(np.asarray(v) for v in (
        x, cond_8, L0_cond_W_up, L0_cond_b_up, L0_cond_W_gate, L0_cond_b_gate, L0_cond_W_down,
        L0_cond_b_down, L1_cond_W_base, L1_cond_b_base, L1_cond_As, L1_cond_Bs)))
    nc = bacc.Bacc("TRN2", target_bir_lowering=False, num_devices=1)
    aps = [nc.dram_tensor(f"{k}_dram", v.shape, F32, kind="ExternalInput").ap() for k, v in arrays.items()]
    out = nc.dram_tensor("out", (B + 1, S, D), F32, kind="ExternalOutput").ap()
    build(nc, *aps, out)
    got = run_bass_kernel_spmd(nc, [{f"{k}_dram": v for k, v in arrays.items()}], core_ids=[0])
    return got.results[0]["out"][:B]
```
